# Optimizing a Trainium2 kernel written in Bass

```python
import numpy as np
import jax
import jax.numpy as jnp

def _softmax(x, axis=-1):
    return jax.nn.softmax(x, axis=axis)

def _gelu(x):
    return jax.nn.gelu(x, approximate=True)

def _silu(x):
    return jax.nn.silu(x)

def _sigmoid(x):
    return jax.nn.sigmoid(x)

def _layernorm(x, axis=-1, eps=1e-05):
    m = jnp.mean(x, axis=axis, keepdims=True)
    v = jnp.var(x, axis=axis, keepdims=True)
    return (x - m) / jnp.sqrt(v + eps)

def _scatter_add(tgt, idx, src, axis=0):
    return tgt.at[idx].add(src)

def _segment_sum(src, seg, n):
    return jax.ops.segment_sum(src, seg, n)
kernel_name = 'mk_dlrm_tower_d1_rec_r8_db037d'

def setup_inputs(seed: int=0):
    np.random.seed(seed)
    _w = jnp.asarray

    def _rec_inputs():
        import jax
        import jax.numpy as jnp
        _tk = jax.random.key(seed)
        dense_ctx = jax.random.normal(jax.random.fold_in(_tk, 190), (2048, 16), jnp.float32)
        ids = jnp.stack([jax.random.randint(jax.random.fold_in(_tk, 200 + f), (2048,), 0, v, jnp.int32) for f, v in enumerate([1000, 1000, 125000, 12500, 1250, 125000, 12500, 1250, 1000, 1250, 1000, 125000, 1000, 1250, 125000, 125000, 125000, 125000, 1250, 12500, 1250, 1000, 125000, 1000, 1000, 1250, 1250, 1000, 125000, 125000, 1250, 1000, 1250, 125000, 12500, 12500, 125000, 1000, 125000])], axis=1)
        tbl_0 = 0.05 * jax.random.normal(jax.random.fold_in(_tk, 500 + 0), (1000, 16), jnp.float32)
        tbl_1 = 0.05 * jax.random.normal(jax.random.fold_in(_tk, 500 + 1), (1000, 16), jnp.float32)
        tbl_2 = 0.05 * jax.random.normal(jax.random.fold_in(_tk, 500 + 2), (125000, 16), jnp.float32)
        tbl_3 = 0.05 * jax.random.normal(jax.random.fold_in(_tk, 500 + 3), (12500, 16), jnp.float32)
        tbl_4 = 0.05 * jax.random.normal(jax.random.fold_in(_tk, 500 + 4), (1250, 16), jnp.float32)
        tbl_5 = 0.05 * jax.random.normal(jax.random.fold_in(_tk, 500 + 5), (125000, 16), jnp.float32)
        tbl_6 = 0.05 * jax.random.normal(jax.random.fold_in(_tk, 500 + 6), (12500, 16), jnp.float32)
        tbl_7 = 0.05 * jax.random.normal(jax.random.fold_in(_tk, 500 + 7), (1250, 16), jnp.float32)
        tbl_8 = 0.05 * jax.random.normal(jax.random.fold_in(_tk, 500 + 8), (1000, 16), jnp.float32)
        tbl_9 = 0.05 * jax.random.normal(jax.random.fold_in(_tk, 500 + 9), (1250, 16), jnp.float32)
        tbl_10 = 0.05 * jax.random.normal(jax.random.fold_in(_tk, 500 + 10), (1000, 16), jnp.float32)
        tbl_11 = 0.05 * jax.random.normal(jax.random.fold_in(_tk, 500 + 11), (125000, 16), jnp.float32)
        tbl_12 = 0.05 * jax.random.normal(jax.random.fold_in(_tk, 500 + 12), (1000, 16), jnp.float32)
        tbl_13 = 0.05 * jax.random.normal(jax.random.fold_in(_tk, 500 + 13), (1250, 16), jnp.float32)
        tbl_14 = 0.05 * jax.random.normal(jax.random.fold_in(_tk, 500 + 14), (125000, 16), jnp.float32)
        tbl_15 = 0.05 * jax.random.normal(jax.random.fold_in(_tk, 500 + 15), (125000, 16), jnp.float32)
        tbl_16 = 0.05 * jax.random.normal(jax.random.fold_in(_tk, 500 + 16), (125000, 16), jnp.float32)
        tbl_17 = 0.05 * jax.random.normal(jax.random.fold_in(_tk, 500 + 17), (125000, 16), jnp.float32)
        tbl_18 = 0.05 * jax.random.normal(jax.random.fold_in(_tk, 500 + 18), (1250, 16), jnp.float32)
        tbl_19 = 0.05 * jax.random.normal(jax.random.fold_in(_tk, 500 + 19), (12500, 16), jnp.float32)
        tbl_20 = 0.05 * jax.random.normal(jax.random.fold_in(_tk, 500 + 20), (1250, 16), jnp.float32)
        tbl_21 = 0.05 * jax.random.normal(jax.random.fold_in(_tk, 500 + 21), (1000, 16), jnp.float32)
        tbl_22 = 0.05 * jax.random.normal(jax.random.fold_in(_tk, 500 + 22), (125000, 16), jnp.float32)
        tbl_23 = 0.05 * jax.random.normal(jax.random.fold_in(_tk, 500 + 23), (1000, 16), jnp.float32)
        tbl_24 = 0.05 * jax.random.normal(jax.random.fold_in(_tk, 500 + 24), (1000, 16), jnp.float32)
        tbl_25 = 0.05 * jax.random.normal(jax.random.fold_in(_tk, 500 + 25), (1250, 16), jnp.float32)
        tbl_26 = 0.05 * jax.random.normal(jax.random.fold_in(_tk, 500 + 26), (1250, 16), jnp.float32)
        tbl_27 = 0.05 * jax.random.normal(jax.random.fold_in(_tk, 500 + 27), (1000, 16), jnp.float32)
        tbl_28 = 0.05 * jax.random.normal(jax.random.fold_in(_tk, 500 + 28), (125000, 16), jnp.float32)
        tbl_29 = 0.05 * jax.random.normal(jax.random.fold_in(_tk, 500 + 29), (125000, 16), jnp.float32)
        tbl_30 = 0.05 * jax.random.normal(jax.random.fold_in(_tk, 500 + 30), (1250, 16), jnp.float32)
        tbl_31 = 0.05 * jax.random.normal(jax.random.fold_in(_tk, 500 + 31), (1000, 16), jnp.float32)
        tbl_32 = 0.05 * jax.random.normal(jax.random.fold_in(_tk, 500 + 32), (1250, 16), jnp.float32)
        tbl_33 = 0.05 * jax.random.normal(jax.random.fold_in(_tk, 500 + 33), (125000, 16), jnp.float32)
        tbl_34 = 0.05 * jax.random.normal(jax.random.fold_in(_tk, 500 + 34), (12500, 16), jnp.float32)
        tbl_35 = 0.05 * jax.random.normal(jax.random.fold_in(_tk, 500 + 35), (12500, 16), jnp.float32)
        tbl_36 = 0.05 * jax.random.normal(jax.random.fold_in(_tk, 500 + 36), (125000, 16), jnp.float32)
        tbl_37 = 0.05 * jax.random.normal(jax.random.fold_in(_tk, 500 + 37), (1000, 16), jnp.float32)
        tbl_38 = 0.05 * jax.random.normal(jax.random.fold_in(_tk, 500 + 38), (125000, 16), jnp.float32)
        _rk = jax.random.fold_in(_tk, 7)
        W_top1 = 0.0693375 * jax.random.normal(jax.random.fold_in(_tk, 801), (208, 512), jnp.float32)
        W_top2 = 0.0441942 * jax.random.normal(jax.random.fold_in(_tk, 802), (512, 256), jnp.float32)
        W_top3 = 0.0625 * jax.random.normal(jax.random.fold_in(_tk, 803), (256, 1), jnp.float32)
        b_top1 = jnp.zeros((512,), jnp.float32)
        b_top2 = jnp.zeros((256,), jnp.float32)
        return (dense_ctx, ids, tbl_0, tbl_1, tbl_2, tbl_3, tbl_4, tbl_5, tbl_6, tbl_7, tbl_8, tbl_9, tbl_10, tbl_11, tbl_12, tbl_13, tbl_14, tbl_15, tbl_16, tbl_17, tbl_18, tbl_19, tbl_20, tbl_21, tbl_22, tbl_23, tbl_24, tbl_25, tbl_26, tbl_27, tbl_28, tbl_29, tbl_30, tbl_31, tbl_32, tbl_33, tbl_34, tbl_35, tbl_36, tbl_37, tbl_38, W_top1, b_top1, W_top2, b_top2, W_top3)
    dense_ctx, ids, tbl_0, tbl_1, tbl_2, tbl_3, tbl_4, tbl_5, tbl_6, tbl_7, tbl_8, tbl_9, tbl_10, tbl_11, tbl_12, tbl_13, tbl_14, tbl_15, tbl_16, tbl_17, tbl_18, tbl_19, tbl_20, tbl_21, tbl_22, tbl_23, tbl_24, tbl_25, tbl_26, tbl_27, tbl_28, tbl_29, tbl_30, tbl_31, tbl_32, tbl_33, tbl_34, tbl_35, tbl_36, tbl_37, tbl_38, W_top1, b_top1, W_top2, b_top2, W_top3 = _rec_inputs()

    def _L0_rec_setup():
        import jax, jax.numpy as jnp
        import numpy as np
        key = jax.random.key(seed)
        k1, k2, k3 = jax.random.split(key, 3)
        B, F0, D = (1024, 39, 16)
        L = 128
        hash_x = jax.random.normal(k1, (B, F0, D), dtype=jnp.float32)
        W0 = jax.random.normal(k2, (F0 * F0, L), dtype=jnp.float32) * 0.05
        W1 = jax.random.normal(k3, (F0 * (L // 2), L), dtype=jnp.float32) * 0.05
        return {'hash_x': hash_x, 'W0': W0, 'W1': W1}
    _L0_rec_all = _L0_rec_setup()
    _L0_rec_in = {k: v for k, v in _L0_rec_all.items() if k in ('W0', 'W1')}
    del _L0_rec_all
    return {'dense_ctx': dense_ctx, 'ids': ids, 'tbl_0': tbl_0, 'tbl_1': tbl_1, 'tbl_2': tbl_2, 'tbl_3': tbl_3, 'tbl_4': tbl_4, 'tbl_5': tbl_5, 'tbl_6': tbl_6, 'tbl_7': tbl_7, 'tbl_8': tbl_8, 'tbl_9': tbl_9, 'tbl_10': tbl_10, 'tbl_11': tbl_11, 'tbl_12': tbl_12, 'tbl_13': tbl_13, 'tbl_14': tbl_14, 'tbl_15': tbl_15, 'tbl_16': tbl_16, 'tbl_17': tbl_17, 'tbl_18': tbl_18, 'tbl_19': tbl_19, 'tbl_20': tbl_20, 'tbl_21': tbl_21, 'tbl_22': tbl_22, 'tbl_23': tbl_23, 'tbl_24': tbl_24, 'tbl_25': tbl_25, 'tbl_26': tbl_26, 'tbl_27': tbl_27, 'tbl_28': tbl_28, 'tbl_29': tbl_29, 'tbl_30': tbl_30, 'tbl_31': tbl_31, 'tbl_32': tbl_32, 'tbl_33': tbl_33, 'tbl_34': tbl_34, 'tbl_35': tbl_35, 'tbl_36': tbl_36, 'tbl_37': tbl_37, 'tbl_38': tbl_38, 'W_top1': W_top1, 'b_top1': b_top1, 'W_top2': W_top2, 'b_top2': b_top2, 'W_top3': W_top3, 'L0_rec_W0': _L0_rec_in['W0'], 'L0_rec_W1': _L0_rec_in['W1']}

def reference(dense_ctx, ids, tbl_0, tbl_1, tbl_2, tbl_3, tbl_4, tbl_5, tbl_6, tbl_7, tbl_8, tbl_9, tbl_10, tbl_11, tbl_12, tbl_13, tbl_14, tbl_15, tbl_16, tbl_17, tbl_18, tbl_19, tbl_20, tbl_21, tbl_22, tbl_23, tbl_24, tbl_25, tbl_26, tbl_27, tbl_28, tbl_29, tbl_30, tbl_31, tbl_32, tbl_33, tbl_34, tbl_35, tbl_36, tbl_37, tbl_38, W_top1, b_top1, W_top2, b_top2, W_top3, L0_rec_W0, L0_rec_W1):
    import jax
    import jax.numpy as jnp

    def _L0_rec_ref(hash_x, W0, W1):
        import jax, jax.numpy as jnp
        import numpy as np
        x0 = hash_x
        B, F0, D = x0.shape
        L = W0.shape[1]
        z0 = jnp.einsum('bid,bjd->bdij', x0, x0).reshape(B, D, F0 * F0)
        cur0 = jax.nn.relu(jnp.einsum('bdk,kl->bld', z0, W0))
        next_h, direct0 = jnp.split(cur0, 2, axis=1)
        Fk = next_h.shape[1]
        z1 = jnp.einsum('bid,bjd->bdij', x0, next_h).reshape(B, D, F0 * Fk)
        cur1 = jax.nn.relu(jnp.einsum('bdk,kl->bld', z1, W1))
        result = jnp.concatenate([direct0, cur1], axis=1)
        return jnp.sum(result, axis=-1)
    e = jnp.stack([tbl_0[ids[:, 0]], tbl_1[ids[:, 1]], tbl_2[ids[:, 2]], tbl_3[ids[:, 3]], tbl_4[ids[:, 4]], tbl_5[ids[:, 5]], tbl_6[ids[:, 6]], tbl_7[ids[:, 7]], tbl_8[ids[:, 8]], tbl_9[ids[:, 9]], tbl_10[ids[:, 10]], tbl_11[ids[:, 11]], tbl_12[ids[:, 12]], tbl_13[ids[:, 13]], tbl_14[ids[:, 14]], tbl_15[ids[:, 15]], tbl_16[ids[:, 16]], tbl_17[ids[:, 17]], tbl_18[ids[:, 18]], tbl_19[ids[:, 19]], tbl_20[ids[:, 20]], tbl_21[ids[:, 21]], tbl_22[ids[:, 22]], tbl_23[ids[:, 23]], tbl_24[ids[:, 24]], tbl_25[ids[:, 25]], tbl_26[ids[:, 26]], tbl_27[ids[:, 27]], tbl_28[ids[:, 28]], tbl_29[ids[:, 29]], tbl_30[ids[:, 30]], tbl_31[ids[:, 31]], tbl_32[ids[:, 32]], tbl_33[ids[:, 33]], tbl_34[ids[:, 34]], tbl_35[ids[:, 35]], tbl_36[ids[:, 36]], tbl_37[ids[:, 37]], tbl_38[ids[:, 38]]], axis=1)
    z = _L0_rec_ref(e, L0_rec_W0, L0_rec_W1)
    z = z.reshape(z.shape[0], -1)
    h = jnp.concatenate([z, dense_ctx], axis=1)
    h = jnp.maximum(h @ W_top1 + b_top1, 0.0)
    h = jnp.maximum(h @ W_top2 + b_top2, 0.0)
    y = h @ W_top3
    return y

_drawn_inputs = setup_inputs


def setup_inputs(seed=0):
    import zlib

    import numpy as np

    out = dict(_drawn_inputs(seed))
    spreads = {'b_top1': (0.0, 0.8), 'b_top2': (0.0, 0.448)}
    factors = {'tbl_0': 8.0,
     'tbl_1': 8.0,
     'tbl_2': 8.0,
     'tbl_3': 8.0,
     'tbl_4': 8.0,
     'tbl_5': 8.0,
     'tbl_6': 8.0,
     'tbl_7': 8.0,
     'tbl_8': 8.0,
     'tbl_9': 8.0,
     'tbl_10': 8.0,
     'tbl_11': 8.0,
     'tbl_12': 8.0,
     'tbl_13': 8.0,
     'tbl_14': 8.0,
     'tbl_15': 8.0,
     'tbl_16': 8.0,
     'tbl_17': 8.0,
     'tbl_18': 8.0,
     'tbl_19': 8.0,
     'tbl_20': 8.0,
     'tbl_21': 8.0,
     'tbl_22': 8.0,
     'tbl_23': 8.0,
     'tbl_24': 8.0,
     'tbl_25': 8.0,
     'tbl_26': 8.0,
     'tbl_27': 8.0,
     'tbl_28': 8.0,
     'tbl_29': 8.0,
     'tbl_30': 8.0,
     'tbl_31': 8.0,
     'tbl_32': 8.0,
     'tbl_33': 8.0,
     'tbl_34': 8.0,
     'tbl_35': 8.0,
     'tbl_36': 8.0,
     'tbl_37': 8.0,
     'tbl_38': 8.0,
     'L0_rec_W1': 8.0}
    for name, (base, spread) in spreads.items():
        noise = np.random.default_rng([zlib.crc32(name.encode()), seed]).standard_normal(out[name].shape)
        drawn = base * np.exp(spread * noise) if base else spread * noise
        out[name] = jnp.asarray(drawn.astype(out[name].dtype))
    for name, factor in factors.items():
        out[name] = (out[name] * factor).astype(out[name].dtype)
    return out
```

```python
import concourse.bass as bass
from concourse import mybir
from contextlib import ExitStack

BATCH, FIELDS, DIM, CH, HALF = 2048, 39, 16, 128, 64
PART = 128
BLOCKS = BATCH // PART
BLOCK_COLS = PART * DIM
STEPS = 2 * BLOCKS
COLS = BLOCK_COLS // 2
DIMS = DIM // 2
BANK = 512
XROWS = 2 * FIELDS

X_BLOCK = XROWS * BLOCK_COLS

SHIFTS = [[34, 14, 30], [8, 5, 1], [15, 28, 30], [11, 0, 9], [33, 2, 24]]
PAIRS0 = [(0, 1), (1, 2), (2, 3), (3, 4), (4, 0), (0, 2), (1, 3)]
K0 = 3 * FIELDS
XT, HT = 5, 4
PAIRS1 = [(t, u) for t in range(XT) for u in range(HT)]
N0, N1 = len(PAIRS0), len(PAIRS1)
PER_STEP = N0 + N1
PER_BLOCK = 2 * PER_STEP
RING = 6
FIRST = 2 * N0

TCH = 5
TLAST = FIELDS * DIM - 4 * PART
H1, H2, CTX = 512, 256, 16
M1, M2 = H1 // PART, H2 // PART
KB = HALF + CTX


def product_at(s):
    return FIRST + PER_STEP * s


def l1_at(s, last):
    return FIRST + PER_STEP * (STEPS - 2) + N1 * (s - STEPS + 2) if last else product_at(s) + N0


def cin_kernel(nc, ids, tables, ctx_t, w0a, w0b, w1, b1, b2, wt1a, wt1b, wt2, wt3, ident, out):
    fp32, i32, u32 = mybir.dt.float32, mybir.dt.int32, mybir.dt.uint32
    ALU, ACT, AX = mybir.AluOpType, mybir.ActivationFunctionType, mybir.AxisListType

    with ExitStack() as ctx:
        def sb(name, shape, dt=fp32):
            return ctx.enter_context(nc.sbuf_tensor(name, shape, dt))

        def ps(name, shape):
            return ctx.enter_context(nc.psum_tensor(name, shape, fp32))

        def sem(name):
            return ctx.enter_context(nc.semaphore(name))

        x_dram = nc.dram_tensor("x_dram", [BLOCKS * XROWS * BLOCK_COLS], fp32, kind="Internal").ap()
        h_dram = nc.dram_tensor("h_dram", [2, HALF, COLS], fp32, kind="Internal").ap()

        ids_sb = sb("ids_sb", [PART, BLOCKS * FIELDS], u32)
        ids_now = sb("ids_now", [PART, FIELDS], u32)
        emb = sb("emb", [PART, FIELDS * DIM])
        emb_t = sb("emb_t", [PART, TCH * PART])
        ident_sb = sb("ident_sb", [PART, PART])
        shift_x = sb("shift_x", [PART, 2, len(SHIFTS), COLS])
        tile_x = sb("tile_x", [PART, 2, XT, COLS])
        tile_h = sb("tile_h", [PART, 2, HT, COLS])
        prod = sb("prod", [PART, RING, COLS])
        cur0 = sb("cur0", [PART, 2, COLS])
        cur1 = sb("cur1", [PART, COLS])
        w0_sb = sb("w0_sb", [K0, N0, CH])
        w1_sb = sb("w1_sb", [PART, N1, CH])
        dsum = sb("dsum", [HALF, 2, PART])
        csum = sb("csum", [PART, 2, PART])
        feat_a = sb("feat_a", [PART, PART])
        feat_b = sb("feat_b", [KB, BATCH])
        wt1a_sb = sb("wt1a_sb", [PART, H1])
        wt1b_sb = sb("wt1b_sb", [KB, H1])
        wt2_sb = sb("wt2_sb", [PART, M1, H2])
        wt3_sb = sb("wt3_sb", [PART, M2])
        b1_sb = sb("b1_sb", [PART, M1])
        b2_sb = sb("b2_sb", [PART, M2])
        hid1 = sb("hid1", [PART, M1, PART])
        hid2 = sb("hid2", [PART, M2, PART])
        y_row = sb("y_row", [1, BATCH])
        w0b_sb = prod[0:K0, 0, 0:N0 * CH].rearrange("p (c l) -> p c l", c=N0)

        acc0 = ps("acc0", [PART, COLS])
        acc1 = ps("acc1", [PART, COLS])
        ps_t = ps("ps_t", [PART, 2, BANK])
        ps_m1 = ps("ps_m1", [PART, M1, PART])
        ps_m2 = ps("ps_m2", [PART, BANK])

        ids_in = sem("ids_in")
        ids_copied = sem("ids_copied")
        gathers_begun = sem("gathers_begun")
        gathered = sem("gathered")
        weights_in = sem("weights_in")
        w0_in = sem("w0_in")
        w0_ready = sem("w0_ready")
        transposed = sem("transposed")
        emb_t_ready = sem("emb_t_ready")
        x_stored = sem("x_stored")
        shift_loaded = [sem("shift_loaded_even"), sem("shift_loaded_odd")]
        tiles_loaded = [sem("tiles_loaded_even"), sem("tiles_loaded_odd")]
        h_stored = [sem("h_stored_even"), sem("h_stored_odd")]
        made = sem("made")
        used = sem("used")
        cur0_ready = sem("cur0_ready")
        cur1_ready = sem("cur1_ready")
        direct_summed = sem("direct_summed")
        cur1_summed = sem("cur1_summed")
        feat_b_ready = sem("feat_b_ready")
        feat_a_ready = sem("feat_a_ready")
        m1_done = sem("m1_done")
        m2_done = sem("m2_done")
        m3_done = sem("m3_done")
        hid1_ready = sem("hid1_ready")
        hid2_ready = sem("hid2_ready")
        y_ready = sem("y_ready")
        y_stored = sem("y_stored")

        SHIFT_SEM = 16 * 3 * len(SHIFTS)
        TILE_SEM = 16 * (XT + HT)
        XST_SEM = 16 * 4
        GATH_SEM = 16 * FIELDS

        block = ctx.enter_context(nc.Block())

        @block.sync
        def _(sp):
            def load_shift(x_at, p):
                base = x_at + p * COLS
                for t, shifts in enumerate(SHIFTS):
                    for q, a in enumerate(shifts):
                        src = bass.AP(x_dram.tensor, base + a * BLOCK_COLS,
                                      [[BLOCK_COLS, FIELDS], [1, COLS]])
                        sp.dma_start(shift_x[q * FIELDS:(q + 1) * FIELDS, p, t, :],
                                     src).then_inc(shift_loaded[p], 16)

            def load_tiles(x_at, p):
                base = x_at + p * COLS
                for u in range(HT):
                    src = bass.AP(h_dram.tensor, p * HALF * COLS + u * 16 * COLS,
                                  [[COLS, 16], [0, 8], [1, COLS]])
                    sp.dma_start(tile_h[:, p, u, :], src).then_inc(tiles_loaded[p], 16)
                for t in range(XT):
                    src = bass.AP(x_dram.tensor, base + t * 8 * BLOCK_COLS,
                                  [[0, 16], [BLOCK_COLS, 8], [1, COLS]])
                    sp.dma_start(tile_x[:, p, t, :], src).then_inc(tiles_loaded[p], 16)

            def store_x(x_at, blocks):
                sp.wait_ge(emb_t_ready, blocks)
                for copy in range(2):
                    base = x_at + copy * FIELDS * BLOCK_COLS
                    full = bass.AP(x_dram.tensor, base, [[PART, PART], [PART * PART, 4], [1, PART]])
                    rest = bass.AP(x_dram.tensor, base + 4 * PART * PART, [[PART, TLAST], [1, PART]])
                    sp.dma_start(full, emb_t[:, 0:4 * PART].rearrange("p (c b) -> p c b", c=4)
                                 ).then_inc(x_stored, 16)
                    sp.dma_start(rest, emb_t[0:TLAST, 4 * PART:]).then_inc(x_stored, 16)

            def store_h(p, steps, tiles_before=0):
                sp.wait_ge(cur0_ready, steps)
                if not isinstance(tiles_before, int) or tiles_before:
                    sp.wait_ge(tiles_loaded[p], tiles_before)
                sp.dma_start(h_dram[p], cur0[HALF:, p, :]).then_inc(h_stored[p], 16)

            sp.dma_start(ids_sb[:, :], ids).then_inc(ids_in, 16)
            sp.dma_start(ident_sb[:, :], ident).then_inc(weights_in, 16)
            sp.dma_start(w0_sb[:, :, :], w0a).then_inc(w0_in, 16)
            sp.dma_start(w0b_sb, w0b).then_inc(w0_in, 16)
            sp.dma_start(w1_sb[:, :, :], w1).then_inc(weights_in, 16)
            sp.dma_start(feat_b[HALF:, :], ctx_t).then_inc(weights_in, 16)
            sp.dma_start(wt1a_sb[:, :], wt1a).then_inc(weights_in, 16)
            sp.dma_start(wt1b_sb[:, :], wt1b).then_inc(weights_in, 16)
            sp.dma_start(wt2_sb[:, :, :], wt2).then_inc(weights_in, 16)
            sp.dma_start(wt3_sb[:, :], wt3).then_inc(weights_in, 16)
            sp.dma_start(b1_sb[:, :], b1).then_inc(weights_in, 16)
            sp.dma_start(b2_sb[:, :], b2).then_inc(weights_in, 16)

            store_x(0, 1)
            sp.wait_ge(x_stored, XST_SEM)
            load_shift(0, 0)
            load_shift(0, 1)
            for p in range(2):
                store_h(p, p + 1)
                sp.wait_ge(h_stored[p], 16)
                load_tiles(0, p)
            store_x(X_BLOCK, 2)
            sp.wait_ge(x_stored, 2 * XST_SEM)
            for p in range(2):
                load_shift(X_BLOCK, p)

            def body(b, more_x):
                value = (lambda v: v if isinstance(v, int) else sp.snap(v))
                x_next, x_after = value((b + 1) * X_BLOCK), value((b + 2) * X_BLOCK)
                tiles_before, stores_after = value(TILE_SEM * (b + 1)), value(16 * (b + 2))
                l1_even, l1_odd = value(l1_at(2 * b, False) + N1), value(l1_at(2 * b + 1, False) + N1)
                relus_even, relus_odd = value(2 * b + 3), value(2 * b + 4)
                emb_blocks, x_stores = value(b + 3), value(XST_SEM * (b + 3))

                store_h(0, relus_even, tiles_before)
                sp.wait_ge(h_stored[0], stores_after)
                sp.wait_ge(made, l1_even)
                load_tiles(x_next, 0)
                if more_x:
                    store_x(x_after, emb_blocks)
                    sp.wait_ge(x_stored, x_stores)
                    load_shift(x_after, 0)
                store_h(1, relus_odd, tiles_before)
                if more_x:
                    load_shift(x_after, 1)
                sp.wait_ge(h_stored[1], stores_after)
                sp.wait_ge(made, l1_odd)
                load_tiles(x_next, 1)

            with sp.Fori(0, BLOCKS - 2) as b:
                body(b, True)
            body(BLOCKS - 2, False)
            sp.wait_ge(y_ready, BLOCKS)
            sp.dma_start(out, y_row[:, :]).then_inc(y_stored, 16)
            sp.wait_ge(y_stored, 16)

        @block.gpsimd
        def _(pool):
            def gather(b, first):
                if not first:
                    pool.wait_ge(gathered, GATH_SEM * b)
                nc.gpsimd.tensor_copy(ids_now[:, :], ids_sb[:, bass.ds(b * FIELDS, FIELDS)]
                                      ).then_inc(ids_copied, 1)
                if not first:
                    pool.wait_ge(transposed, b)
                pool.wait_ge(ids_copied, b + 1)
                pool.sem_inc(gathers_begun, 1)
                for f in range(FIELDS):
                    nc.gpsimd.indirect_dma_start(
                        out=emb[:, f * DIM:(f + 1) * DIM], out_offset=None, in_=tables[f],
                        in_offset=bass.IndirectOffsetOnAxis(ap=ids_now[:, f:f + 1], axis=0),
                    ).then_inc(gathered, 16)

            pool.wait_ge(ids_in, 16)
            gather(0, True)
            with pool.Fori(1, BLOCKS) as b:
                gather(b, False)

        @block.scalar
        def _(act):
            def relu0(b, p, l0_end, first=False):
                act.wait_ge(used, l0_end)
                if not first:
                    act.wait_ge(direct_summed, 2 * b + p - 1)
                    act.wait_ge(h_stored[p], 16 * b)
                nc.scalar.activation(cur0[:, p, :], acc0[:, :], ACT.Relu).then_inc(cur0_ready, 1)

            def relu1(b, p, l1_end, first=False):
                act.wait_ge(used, l1_end)
                if not first:
                    act.wait_ge(cur1_summed, 2 * b + p)
                nc.scalar.activation(cur1[:, :], acc1[:, :], ACT.Relu).then_inc(cur1_ready, 1)

            def evacuate(b, first):
                act.wait_ge(transposed, b + 1)
                if not first:
                    act.wait_ge(x_stored, XST_SEM * b)
                nc.scalar.activation(emb_t[:, 0:4 * PART], ps_t[:, 0, :], ACT.Copy)
                nc.scalar.activation(emb_t[0:TLAST, 4 * PART:], ps_t[0:TLAST, 1, 0:PART],
                                     ACT.Copy).then_inc(emb_t_ready, 1)

            def hidden1(b):
                act.wait_ge(m1_done, b + 1)
                for m in range(M1):
                    last = nc.scalar.activation(hid1[:, m, :], ps_m1[:, m, :], ACT.Relu,
                                                bias=b1_sb[:, m:m + 1])
                last.then_inc(hid1_ready, 1)

            def hidden2(b):
                act.wait_ge(m2_done, b + 1)
                for m in range(M2):
                    last = nc.scalar.activation(hid2[:, m, :], ps_m2[:, m * PART:(m + 1) * PART],
                                                ACT.Relu, bias=b2_sb[:, m:m + 1])
                last.then_inc(hid2_ready, 1)

            def score(b):
                act.wait_ge(m3_done, b + 1)
                nc.scalar.activation(y_row[:, bass.ds(b * PART, PART)], ps_m2[0:1, 3 * PART:],
                                     ACT.Copy).then_inc(y_ready, 1)

            evacuate(0, True)
            relu0(0, 0, N0, True)
            relu0(0, 1, 2 * N0, True)
            evacuate(1, False)
            act.wait_ge(weights_in, 16 * 9)

            def body(b, more_x, more_h, mlp, first=False):
                n = FIRST + PER_BLOCK * b
                if more_h:
                    n = n + N0
                    relu0(b + 1, 0, n)
                n = n + N1
                relu1(b, 0, n, first)
                if more_x:
                    evacuate(b + 2, False)
                if mlp:
                    hidden1(b - 1)
                if more_h:
                    n = n + N0
                    relu0(b + 1, 1, n)
                if mlp:
                    hidden2(b - 1)
                    score(b - 1)
                relu1(b, 1, n + N1)

            body(0, True, True, False, True)
            with act.Fori(1, BLOCKS - 2) as b:
                body(b, True, True, True)
            body(BLOCKS - 2, False, True, True)
            body(BLOCKS - 1, False, False, True)
            hidden1(BLOCKS - 1)
            hidden2(BLOCKS - 1)
            score(BLOCKS - 1)

        @block.vector
        def _(dve):
            def multiply(n, slot, a, b, rows):
                if isinstance(n, int) and n < RING:
                    pass
                else:
                    dve.wait_ge(used, n + 1 - RING)
                nc.vector.tensor_tensor(prod[0:rows, slot, :], a, b, ALU.mult).then_inc(made, 1)

            def layer0(b, p, n, slot):
                dve.wait_ge(shift_loaded[p], SHIFT_SEM * (b + 1))
                for c, (t, u) in enumerate(PAIRS0):
                    multiply(n + c, (slot + c) % RING, shift_x[0:K0, p, t, :],
                             shift_x[0:K0, p, u, :], K0)

            def layer1(b, p, n, slot, sums):
                dve.wait_ge(tiles_loaded[p], TILE_SEM * (b + 1))
                for c, (t, u) in enumerate(PAIRS1):
                    multiply(n + c, (slot + c) % RING, tile_x[:, p, t, :], tile_h[:, p, u, :], PART)
                    if c == N1 // 2:
                        sums()

            def sum_direct(b, p):
                dve.wait_ge(cur0_ready, 2 * b + p + 1)
                nc.vector.tensor_reduce(
                    dsum[:, p, :], cur0[0:HALF, p, :].rearrange("l (d b) -> l b d", d=DIMS),
                    AX.X, ALU.add).then_inc(direct_summed, 1)
                if p:
                    dve.wait_ge(direct_summed, 2 * b + 2)
                    nc.vector.tensor_tensor(feat_b[0:HALF, bass.ds(b * PART, PART)], dsum[:, 0, :],
                                            dsum[:, 1, :], ALU.add).then_inc(feat_b_ready, 1)

            def sum_cur1(b, p, first=False):
                dve.wait_ge(cur1_ready, 2 * b + p + 1)
                nc.vector.tensor_reduce(
                    csum[:, p, :], cur1[:, :].rearrange("l (d b) -> l b d", d=DIMS),
                    AX.X, ALU.add).then_inc(cur1_summed, 1)
                if p:
                    dve.wait_ge(cur1_summed, 2 * b + 2)
                    if not first:
                        dve.wait_ge(m1_done, b)
                    nc.vector.tensor_tensor(feat_a[:, :], csum[:, 0, :], csum[:, 1, :],
                                            ALU.add).then_inc(feat_a_ready, 1)

            dve.wait_ge(w0_in, 32)
            nc.vector.tensor_tensor(w0_sb[:, :, :], w0_sb[:, :, :], w0b_sb, ALU.add).then_inc(w0_ready, 1)
            dve.wait_ge(w0_ready, 1)
            layer0(0, 0, 0, 0)
            layer0(0, 1, N0, N0)
            sum_direct(0, 0)
            sum_direct(0, 1)

            def body(b, more_h, first=False):
                n = FIRST + PER_BLOCK * b
                slot = FIRST
                for p in range(2):
                    if more_h:
                        layer0(b + 1, p, n, slot)
                        n, slot = n + N0, slot + N0

                    def sums():
                        if more_h:
                            sum_direct(b + 1, p)
                        if p == 1:
                            sum_cur1(b, 0)
                        elif not first:
                            sum_cur1(b - 1, 1, False)

                    layer1(b, p, n, slot, sums)
                    n, slot = n + N1, slot + N1

            body(0, True, True)
            body(1, True)
            with dve.Fori(2, BLOCKS - 1) as b:
                body(b, True)
            body(BLOCKS - 1, False)
            sum_cur1(BLOCKS - 1, 1)

        @block.tensor
        def _(pe):
            def transpose(b):
                pe.wait_ge(gathered, GATH_SEM * (b + 1))
                if not (isinstance(b, int) and b == 0):
                    pe.wait_ge(emb_t_ready, b)
                for c in range(TCH):
                    m = PART if c < TCH - 1 else TLAST
                    last = nc.tensor.transpose(ps_t[0:m, c // 4, c % 4 * PART:(c % 4 + 1) * PART],
                                               emb[:, c * PART:c * PART + m], ident_sb[:, :])
                last.then_inc(transposed, 1)

            def layer0(b, p, n, slot, first=False):
                if not first:
                    pe.wait_ge(cur0_ready, 2 * b + p)
                for c in range(N0):
                    pe.wait_ge(made, n + c + 1)
                    for half in range(COLS // BANK):
                        cols = slice(half * BANK, (half + 1) * BANK)
                        last = nc.tensor.matmul(acc0[:, cols], w0_sb[:, c, :],
                                                prod[0:K0, (slot + c) % RING, cols],
                                                start=(c == 0), stop=(c == N0 - 1))
                    last.then_inc(used, 1)

            def layer1(b, p, n, slot, first=False):
                if not first:
                    pe.wait_ge(cur1_ready, 2 * b + p)
                for c in range(N1):
                    pe.wait_ge(made, n + c + 1)
                    for half in range(COLS // BANK):
                        cols = slice(half * BANK, (half + 1) * BANK)
                        last = nc.tensor.matmul(acc1[:, cols], w1_sb[:, c, :],
                                                prod[:, (slot + c) % RING, cols],
                                                start=(c == 0), stop=(c == N1 - 1))
                    last.then_inc(used, 1)

            def mlp1(b):
                pe.wait_ge(feat_a_ready, b + 1)
                pe.wait_ge(feat_b_ready, b + 1)
                if not (isinstance(b, int) and b == 0):
                    pe.wait_ge(hid1_ready, b)
                for m in range(M1):
                    cols = slice(m * PART, (m + 1) * PART)
                    nc.tensor.matmul(ps_m1[:, m, :], wt1a_sb[:, cols], feat_a[:, :],
                                     start=True, stop=False)
                    last = nc.tensor.matmul(ps_m1[:, m, :], wt1b_sb[:, cols],
                                            feat_b[:, bass.ds(b * PART, PART)],
                                            start=False, stop=True)
                last.then_inc(m1_done, 1)

            def mlp2(b):
                pe.wait_ge(hid1_ready, b + 1)
                if not (isinstance(b, int) and b == 0):
                    pe.wait_ge(y_ready, b)
                for m in range(M2):
                    for k in range(M1):
                        last = nc.tensor.matmul(ps_m2[:, m * PART:(m + 1) * PART],
                                                wt2_sb[:, k, m * PART:(m + 1) * PART],
                                                hid1[:, k, :], start=(k == 0), stop=(k == M1 - 1))
                last.then_inc(m2_done, 1)

            def mlp3(b):
                pe.wait_ge(hid2_ready, b + 1)
                for k in range(M2):
                    last = nc.tensor.matmul(ps_m2[0:1, 3 * PART:], wt3_sb[:, k:k + 1], hid2[:, k, :],
                                            start=(k == 0), stop=(k == M2 - 1))
                last.then_inc(m3_done, 1)

            pe.wait_ge(weights_in, 16 * 9)
            transpose(0)
            pe.wait_ge(w0_ready, 1)
            layer0(0, 0, 0, 0, True)
            layer0(0, 1, N0, N0)
            transpose(1)

            def body(b, more_x, more_h, mlp, first=False):
                n = FIRST + PER_BLOCK * b
                slot = FIRST
                for p in range(2):
                    if more_h:
                        layer0(b + 1, p, n, slot)
                        n, slot = n + N0, slot + N0
                    if p and mlp:
                        mlp2(b - 1)
                    layer1(b, p, n, slot, first and p == 0)
                    n, slot = n + N1, slot + N1
                    if p == 0:
                        if more_x:
                            transpose(b + 2)
                        if mlp:
                            mlp1(b - 1)
                    elif mlp:
                        mlp3(b - 1)

            body(0, True, True, False, True)
            with pe.Fori(1, BLOCKS - 2) as b:
                body(b, True, True, True)
            body(BLOCKS - 2, False, True, True)
            body(BLOCKS - 1, False, False, True)
            mlp1(BLOCKS - 1)
            mlp2(BLOCKS - 1)
            mlp3(BLOCKS - 1)


def w0_rows():
    import numpy as np
    first = np.full((K0, N0), -1)
    second = np.full((K0, N0), -1)
    seen = set()
    for c, (t, u) in enumerate(PAIRS0):
        for q in range(3):
            for r in range(FIELDS):
                i, j = (r + SHIFTS[t][q]) % FIELDS, (r + SHIFTS[u][q]) % FIELDS
                if (min(i, j), max(i, j)) in seen:
                    continue
                seen.add((min(i, j), max(i, j)))
                first[q * FIELDS + r, c] = i * FIELDS + j
                if i != j:
                    second[q * FIELDS + r, c] = j * FIELDS + i
    assert len(seen) == FIELDS * (FIELDS + 1) // 2
    return first, second


def kernel(**inputs):
    import numpy as np
    import concourse.bacc as bacc
    from concourse.bass_utils import run_bass_kernel_spmd

    def rows_of(w, at):
        padded = np.concatenate([w, np.zeros((1, w.shape[1]), w.dtype)])
        return np.ascontiguousarray(padded[at])

    a = {k: np.asarray(v) for k, v in inputs.items()}
    ids = np.ascontiguousarray(a["ids"].reshape(BLOCKS, PART, FIELDS).transpose(1, 0, 2)).reshape(PART, -1).view(np.uint32)
    w0 = np.concatenate([a["L0_rec_W0"][:, HALF:], a["L0_rec_W0"][:, :HALF]], axis=1)
    first, second = w0_rows()
    r = np.arange(PART)
    w1_at = np.stack([np.where(8 * t + r % 8 < FIELDS, (8 * t + r % 8) * HALF + 16 * u + r // 8, -1)
                      for t, u in PAIRS1], axis=1)
    wt1 = a["W_top1"]
    arrays = {
        "ids": ids,
        "ctx_t": np.ascontiguousarray(a["dense_ctx"].T),
        "w0a": rows_of(w0, first),
        "w0b": rows_of(w0, second),
        "w1": rows_of(a["L0_rec_W1"], w1_at),
        "b1": np.ascontiguousarray(a["b_top1"].reshape(M1, PART).T),
        "b2": np.ascontiguousarray(a["b_top2"].reshape(M2, PART).T),
        "wt1a": np.ascontiguousarray(wt1[HALF:HALF + CH]),
        "wt1b": np.concatenate([wt1[:HALF], wt1[HALF + CH:]]),
        "wt2": np.ascontiguousarray(a["W_top2"].reshape(M1, PART, H2).transpose(1, 0, 2)),
        "wt3": np.ascontiguousarray(a["W_top3"].reshape(M2, PART).T),
        "ident": np.eye(PART, dtype=np.float32),
    }
    nc = bacc.Bacc("TRN2", target_bir_lowering=False, num_devices=1)
    fed, aps = {}, {}
    for name, x in list(arrays.items()) + [(f"tbl_{f}", a[f"tbl_{f}"]) for f in range(FIELDS)]:
        fed[f"in_{name}"] = x
        aps[name] = nc.dram_tensor(f"in_{name}", x.shape, mybir.dt.from_np(x.dtype), kind="ExternalInput").ap()
    out = nc.dram_tensor("out_y", (1, BATCH), mybir.dt.float32, kind="ExternalOutput").ap()
    tables = [aps.pop(f"tbl_{f}") for f in range(FIELDS)]
    cin_kernel(nc, tables=tables, out=out, **aps)
    got = run_bass_kernel_spmd(nc, [fed], core_ids=[0])
    return got.results[0]["out_y"].reshape(BATCH, 1)
```

```python
import concourse.bass as bass
from concourse import mybir
from contextlib import ExitStack

BATCH, FIELDS, DIM, CH, HALF = 2048, 39, 16, 128, 64
PART = 128
BLOCKS = BATCH // PART
BLOCK_COLS = PART * DIM
STEPS = 2 * BLOCKS
COLS = BLOCK_COLS // 2
DIMS = DIM // 2
BANK = 512
XROWS = 2 * FIELDS

X_BLOCK = XROWS * BLOCK_COLS

SHIFTS = [[34, 14, 30], [8, 5, 1], [15, 28, 30], [11, 0, 9], [33, 2, 24]]
PAIRS0 = [(0, 1), (1, 2), (2, 3), (3, 4), (4, 0), (0, 2), (1, 3)]
K0 = 3 * FIELDS
XT, HT = 5, 4
PAIRS1 = [(t, u) for t in range(XT) for u in range(HT)]
N0, N1 = len(PAIRS0), len(PAIRS1)
PER_STEP = N0 + N1
PER_BLOCK = 2 * PER_STEP
RING = 6
FIRST = 2 * N0
SPLIT = [[1, 3, 5, 7, 9, 11, 13, 15, 17], [1, 3, 5, 7, 9, 11, 13, 15, 17]]
HIGHS, LOWS = 3, 2
SPLIT_AT = [0, len(SPLIT[0])]
NSPLIT = len(SPLIT[0]) + len(SPLIT[1])
EITHER = sorted(set(SPLIT[0]) | set(SPLIT[1]))
LAG = 2
assert PER_BLOCK % RING == 0 and NSPLIT % (HIGHS * LOWS) == 0 and EITHER[-1] + LAG < N1
WHOLE = [c for c in range(N1) if c not in EITHER or c not in SPLIT[0] or c not in SPLIT[1]]
MID = N1 // 2

TCH = 5
TLAST = FIELDS * DIM - 4 * PART
H1, H2, CTX = 512, 256, 16
M1, M2 = H1 // PART, H2 // PART
KB = HALF + CTX


def cin_kernel(nc, ids, tables, ctx_t, w0a, w0b, w1, w1s, b1, b2, wt1a, wt1b, wt2, wt3, ident, out):
    fp32, fp32r, u32 = mybir.dt.float32, mybir.dt.float32r, mybir.dt.uint32
    ALU, ACT, AX = mybir.AluOpType, mybir.ActivationFunctionType, mybir.AxisListType

    with ExitStack() as ctx:
        def sb(name, shape, dt=fp32):
            return ctx.enter_context(nc.sbuf_tensor(name, shape, dt))

        def ps(name, shape):
            return ctx.enter_context(nc.psum_tensor(name, shape, fp32))

        def sem(name):
            return ctx.enter_context(nc.semaphore(name))

        x_dram = nc.dram_tensor("x_dram", [BLOCKS * XROWS * BLOCK_COLS], fp32, kind="Internal").ap()
        h_dram = nc.dram_tensor("h_dram", [2, HALF, COLS], fp32, kind="Internal").ap()

        ids_now = sb("ids_now", [PART, FIELDS], u32)
        emb = sb("emb", [PART, FIELDS * DIM])
        emb_t = sb("emb_t", [PART, TCH * PART])
        ident_sb = sb("ident_sb", [PART, PART])
        shift_x = sb("shift_x", [PART, 2, len(SHIFTS), COLS])
        tile_x = sb("tile_x", [PART, 2, XT, COLS])
        tile_h = sb("tile_h", [PART, 2, HT, COLS])
        prod = sb("prod", [PART, RING, COLS])
        high = sb("high", [PART, HIGHS, COLS], fp32r)
        low = sb("low", [PART, LOWS, COLS], fp32r)
        cur0 = sb("cur0", [PART, 2, COLS])
        cur1 = sb("cur1", [PART, COLS])
        w0_sb = sb("w0_sb", [K0, N0, CH])
        w1_sb = sb("w1_sb", [PART, len(WHOLE), CH])
        w1_high = sb("w1_high", [PART, len(EITHER), CH], fp32r)
        w1_low = sb("w1_low", [PART, len(EITHER), CH], fp32r)
        dsum = sb("dsum", [HALF, 2, PART])
        csum = sb("csum", [PART, 2, PART])
        feat_a = sb("feat_a", [PART, PART])
        feat_b = sb("feat_b", [KB, PART])
        wt1a_sb = sb("wt1a_sb", [PART, H1])
        wt1b_sb = sb("wt1b_sb", [KB, H1])
        wt2_sb = sb("wt2_sb", [PART, M1, H2])
        wt3_sb = sb("wt3_sb", [PART, M2])
        b1_sb = sb("b1_sb", [PART, M1])
        b2_sb = sb("b2_sb", [PART, M2])
        hid1 = sb("hid1", [PART, M1, PART])
        hid2 = sb("hid2", [PART, M2, PART])
        y_now = sb("y_now", [1, PART])
        w0b_sb = prod[0:K0, 0, 0:N0 * CH].rearrange("p (c l) -> p c l", c=N0)
        w1s_sb = prod[:, 1:3, :].rearrange("p a (c l) -> p (a c) l", l=CH)[:, 0:len(EITHER), :]

        acc0 = ps("acc0", [PART, COLS])
        acc1 = ps("acc1", [PART, COLS])
        ps_t = ps("ps_t", [PART, 2, BANK])
        ps_m1 = ps("ps_m1", [PART, M1, PART])
        ps_m2 = ps("ps_m2", [PART, BANK])

        ids_in = sem("ids_in")
        gathers_begun = sem("gathers_begun")
        gathered = sem("gathered")
        weights_in = sem("weights_in")
        w0_in = sem("w0_in")
        w0_ready = sem("w0_ready")
        transposed = sem("transposed")
        emb_t_ready = sem("emb_t_ready")
        x_stored = sem("x_stored")
        shift_loaded = [sem("shift_loaded_even"), sem("shift_loaded_odd")]
        tiles_loaded = [sem("tiles_loaded_even"), sem("tiles_loaded_odd")]
        h_stored = [sem("h_stored_even"), sem("h_stored_odd")]
        made = sem("made")
        used = sem("used")
        high_made = sem("high_made")
        low_made = sem("low_made")
        w1_in = sem("w1_in")
        context_in = sem("context_in")
        w1_high_ready = sem("w1_high_ready")
        w1_low_ready = sem("w1_low_ready")
        cur0_ready = sem("cur0_ready")
        cur1_ready = sem("cur1_ready")
        direct_summed = sem("direct_summed")
        cur1_summed = sem("cur1_summed")
        feat_b_ready = sem("feat_b_ready")
        feat_a_ready = sem("feat_a_ready")
        m1_done = sem("m1_done")
        m2_done = sem("m2_done")
        m3_done = sem("m3_done")
        hid1_ready = sem("hid1_ready")
        hid2_ready = sem("hid2_ready")
        y_ready = sem("y_ready")
        y_stored = sem("y_stored")

        SHIFT_SEM = 16 * 3 * len(SHIFTS)
        TILE_SEM = 16 * (XT + HT)
        XST_SEM = 16 * 4
        GATH_SEM = 16 * FIELDS

        block = ctx.enter_context(nc.Block())

        @block.sync
        def _(sp):
            def load_shift(x_at, p):
                base = x_at + p * COLS
                for t, shifts in enumerate(SHIFTS):
                    for q, a in enumerate(shifts):
                        src = bass.AP(x_dram.tensor, base + a * BLOCK_COLS,
                                      [[BLOCK_COLS, FIELDS], [1, COLS]])
                        sp.dma_start(shift_x[q * FIELDS:(q + 1) * FIELDS, p, t, :],
                                     src).then_inc(shift_loaded[p], 16)

            def load_tiles(x_at, p):
                base = x_at + p * COLS
                for u in range(HT):
                    src = bass.AP(h_dram.tensor, p * HALF * COLS + u * 16 * COLS,
                                  [[COLS, 16], [0, 8], [1, COLS]])
                    sp.dma_start(tile_h[:, p, u, :], src).then_inc(tiles_loaded[p], 16)
                for t in range(XT):
                    src = bass.AP(x_dram.tensor, base + t * 8 * BLOCK_COLS,
                                  [[0, 16], [BLOCK_COLS, 8], [1, COLS]])
                    sp.dma_start(tile_x[:, p, t, :], src).then_inc(tiles_loaded[p], 16)

            def store_x(x_at, blocks):
                sp.wait_ge(emb_t_ready, blocks)
                for copy in range(2):
                    base = x_at + copy * FIELDS * BLOCK_COLS
                    full = bass.AP(x_dram.tensor, base, [[PART, PART], [PART * PART, 4], [1, PART]])
                    rest = bass.AP(x_dram.tensor, base + 4 * PART * PART, [[PART, TLAST], [1, PART]])
                    sp.dma_start(full, emb_t[:, 0:4 * PART].rearrange("p (c b) -> p c b", c=4)
                                 ).then_inc(x_stored, 16)
                    sp.dma_start(rest, emb_t[0:TLAST, 4 * PART:]).then_inc(x_stored, 16)

            def load_context(at, blocks):
                if not isinstance(blocks, int) or blocks:
                    sp.wait_ge(m1_done, blocks)
                sp.dma_start(feat_b[HALF:, :], ctx_t[:, bass.ds(at, PART)]).then_inc(context_in, 16)

            def store_h(p, steps):
                sp.wait_ge(cur0_ready, steps)
                sp.dma_start(h_dram[p], cur0[HALF:, p, :]).then_inc(h_stored[p], 16)

            sp.dma_start(ident_sb[:, :], ident).then_inc(weights_in, 16)
            sp.dma_start(w0_sb[:, :, :], w0a).then_inc(w0_in, 16)
            sp.dma_start(w0b_sb, w0b).then_inc(w0_in, 16)
            sp.dma_start(w1s_sb, w1s).then_inc(w1_in, 16)
            sp.dma_start(w1_sb[:, :, :], w1).then_inc(weights_in, 16)
            sp.dma_start(wt1a_sb[:, :], wt1a).then_inc(weights_in, 16)
            sp.dma_start(wt1b_sb[:, :], wt1b).then_inc(weights_in, 16)
            sp.dma_start(wt2_sb[:, :, :], wt2).then_inc(weights_in, 16)
            sp.dma_start(wt3_sb[:, :], wt3).then_inc(weights_in, 16)
            sp.dma_start(b1_sb[:, :], b1).then_inc(weights_in, 16)
            sp.dma_start(b2_sb[:, :], b2).then_inc(weights_in, 16)

            store_x(0, 1)
            sp.wait_ge(x_stored, XST_SEM)
            load_shift(0, 0)
            load_shift(0, 1)
            store_h(0, 1)
            sp.wait_ge(h_stored[0], 16)
            load_tiles(0, 0)
            store_x(X_BLOCK, 2)
            sp.wait_ge(x_stored, 2 * XST_SEM)
            load_shift(X_BLOCK, 0)

            def body(b, more_x, more_h):
                value = (lambda v: v if isinstance(v, int) else sp.snap(v))
                x_now, x_next = value(b * X_BLOCK), value((b + 1) * X_BLOCK)
                x_after = value((b + 2) * X_BLOCK)
                stores_odd, stores_even = value(16 * (b + 1)), value(16 * (b + 2))
                relus_odd, relus_even = value(2 * b + 2), value(2 * b + 3)
                emb_blocks, x_stores = value(b + 3), value(XST_SEM * (b + 3))
                context_at = value(b * PART)

                store_h(1, relus_odd)
                if more_h:
                    load_shift(x_next, 1)
                sp.wait_ge(h_stored[1], stores_odd)
                load_tiles(x_now, 1)
                if more_h:
                    store_h(0, relus_even)
                    sp.wait_ge(h_stored[0], stores_even)
                    load_tiles(x_next, 0)
                if more_x:
                    store_x(x_after, emb_blocks)
                    sp.wait_ge(x_stored, x_stores)
                    load_shift(x_after, 0)
                load_context(context_at, b)

            body(0, True, True)
            with sp.Fori(1, BLOCKS - 2) as b:
                body(b, True, True)
            body(BLOCKS - 2, False, True)
            body(BLOCKS - 1, False, False)

        @block.gpsimd
        def _(pool):
            def gather(b, first):
                if not first:
                    pool.wait_ge(gathered, GATH_SEM * b)
                pool.dma_start(ids_now[:, :], ids[:, bass.ds(b * FIELDS, FIELDS)]).then_inc(ids_in, 16)
                if not first:
                    pool.wait_ge(transposed, b)
                pool.wait_ge(ids_in, 16 * (b + 1))
                pool.sem_inc(gathers_begun, 1)
                for f in range(FIELDS):
                    nc.gpsimd.indirect_dma_start(
                        out=emb[:, f * DIM:(f + 1) * DIM], out_offset=None, in_=tables[f],
                        in_offset=bass.IndirectOffsetOnAxis(ap=ids_now[:, f:f + 1], axis=0),
                    ).then_inc(gathered, 16)

            gather(0, True)
            with pool.Fori(1, BLOCKS) as b:
                gather(b, False)

        @block.scalar
        def _(act):
            def relu0(b, p, l0_end, first=False):
                act.wait_ge(used, l0_end)
                if not first:
                    act.wait_ge(direct_summed, 2 * b + p - 1)
                    act.wait_ge(h_stored[p], 16 * b)
                nc.scalar.activation(cur0[:, p, :], acc0[:, :], ACT.Relu).then_inc(cur0_ready, 1)

            def relu1(b, p, l1_end, first=False):
                act.wait_ge(used, l1_end)
                if not first:
                    act.wait_ge(cur1_summed, 2 * b + p)
                nc.scalar.activation(cur1[:, :], acc1[:, :], ACT.Relu).then_inc(cur1_ready, 1)

            def evacuate(b, first):
                act.wait_ge(transposed, b + 1)
                if not first:
                    act.wait_ge(x_stored, XST_SEM * b)
                nc.scalar.activation(emb_t[:, 0:4 * PART], ps_t[:, 0, :], ACT.Copy)
                nc.scalar.activation(emb_t[0:TLAST, 4 * PART:], ps_t[0:TLAST, 1, 0:PART],
                                     ACT.Copy).then_inc(emb_t_ready, 1)

            def hidden1(b):
                act.wait_ge(m1_done, b + 1)
                for m in range(M1):
                    last = nc.scalar.activation(hid1[:, m, :], ps_m1[:, m, :], ACT.Relu,
                                                bias=b1_sb[:, m:m + 1])
                last.then_inc(hid1_ready, 1)

            def hidden2(b):
                act.wait_ge(m2_done, b + 1)
                for m in range(M2):
                    last = nc.scalar.activation(hid2[:, m, :], ps_m2[:, m * PART:(m + 1) * PART],
                                                ACT.Relu, bias=b2_sb[:, m:m + 1])
                last.then_inc(hid2_ready, 1)

            def score(b):
                act.wait_ge(m3_done, b + 1)
                if not (isinstance(b, int) and b == 0):
                    act.wait_ge(y_stored, 16 * b)
                nc.scalar.activation(y_now[:, :], ps_m2[0:1, 3 * PART:],
                                     ACT.Copy).then_inc(y_ready, 1)
                act.wait_ge(y_ready, b + 1)
                act.dma_start(out[:, bass.ds(b * PART, PART)], y_now[:, :]).then_inc(y_stored, 16)

            def round_high(p, n, slot, which):
                for k in which:
                    c, part = SPLIT[p][k], (SPLIT_AT[p] + k) % HIGHS
                    act.wait_ge(made, n + c + 1)
                    if k >= HIGHS and SPLIT[p][k] - SPLIT[p][k - HIGHS] < RING:
                        act.wait_ge(used, n + SPLIT[p][k - HIGHS] + 1)
                    nc.scalar.activation(high[:, part, :], prod[:, (slot + c) % RING, :],
                                         ACT.Copy).then_inc(high_made, 1)

            evacuate(0, True)
            relu0(0, 0, N0, True)
            evacuate(1, False)
            act.wait_ge(weights_in, 16 * 8)

            def body(b, more_x, more_h, mlp, first=False):
                n = FIRST + PER_BLOCK * b
                slot = FIRST
                count = [len(SPLIT[0]), len(SPLIT[1])]
                round_high(0, n, slot, range(2))
                relu0(b, 1, n, first)
                round_high(0, n, slot, range(2, count[0]))
                n, slot = n + N1, slot + N1
                relu1(b, 0, n, first)
                if more_h:
                    round_high(1, n + N0, slot + N0, range(2))
                    n, slot = n + N0, slot + N0
                    relu0(b + 1, 0, n)
                else:
                    round_high(1, n, slot, range(2))
                if more_x:
                    evacuate(b + 2, False)
                if mlp:
                    hidden1(b - 1)
                round_high(1, n, slot, range(2, 6))
                if mlp:
                    hidden2(b - 1)
                round_high(1, n, slot, range(6, count[1]))
                relu1(b, 1, n + N1)
                if mlp:
                    score(b - 1)

            body(0, True, True, False, True)
            body(1, True, True, True)
            with act.Fori(2, BLOCKS - 2) as b:
                body(b, True, True, True)
            body(BLOCKS - 2, False, True, True)
            body(BLOCKS - 1, False, False, True)
            hidden1(BLOCKS - 1)
            hidden2(BLOCKS - 1)
            score(BLOCKS - 1)
            act.wait_ge(y_stored, 16 * BLOCKS)

        @block.vector
        def _(dve):
            def multiply(n, slot, a, b, rows):
                if isinstance(n, int) and n < RING:
                    pass
                else:
                    dve.wait_ge(used, n + 1 - RING)
                nc.vector.tensor_tensor(prod[0:rows, slot, :], a, b, ALU.mult).then_inc(made, 1)

            def layer0(b, p, n, slot):
                dve.wait_ge(shift_loaded[p], SHIFT_SEM * (b + 1))
                for c, (t, u) in enumerate(PAIRS0):
                    multiply(n + c, (slot + c) % RING, shift_x[0:K0, p, t, :],
                             shift_x[0:K0, p, u, :], K0)

            def subtract(p, k, n, slot, splits):
                c, at = SPLIT[p][k], SPLIT_AT[p] + k
                dve.wait_ge(high_made, splits + k + 1)
                nc.vector.tensor_tensor(low[:, at % LOWS, :], prod[:, (slot + c) % RING, :],
                                        high[:, at % HIGHS, :].bitcast(fp32),
                                        ALU.subtract).then_inc(low_made, 1)

            def layer1(b, p, n, slot, splits, sums):
                dve.wait_ge(tiles_loaded[p], TILE_SEM * (b + 1))
                for c, (t, u) in enumerate(PAIRS1):
                    multiply(n + c, (slot + c) % RING, tile_x[:, p, t, :], tile_h[:, p, u, :], PART)
                    if c - LAG in SPLIT[p]:
                        subtract(p, SPLIT[p].index(c - LAG), n, slot, splits)
                    if c == MID:
                        sums()

            def sum_direct(b, p):
                dve.wait_ge(cur0_ready, 2 * b + p + 1)
                nc.vector.tensor_reduce(
                    dsum[:, p, :], cur0[0:HALF, p, :].rearrange("l (d b) -> l b d", d=DIMS),
                    AX.X, ALU.add).then_inc(direct_summed, 1)

            def join_direct(b):
                dve.wait_ge(direct_summed, 2 * b + 2)
                if not (isinstance(b, int) and b == 0):
                    dve.wait_ge(m1_done, b)
                nc.vector.tensor_tensor(feat_b[0:HALF, :], dsum[:, 0, :], dsum[:, 1, :],
                                        ALU.add).then_inc(feat_b_ready, 1)

            def sum_cur1(b, p):
                dve.wait_ge(cur1_ready, 2 * b + p + 1)
                nc.vector.tensor_reduce(
                    csum[:, p, :], cur1[:, :].rearrange("l (d b) -> l b d", d=DIMS),
                    AX.X, ALU.add).then_inc(cur1_summed, 1)
                if p:
                    dve.wait_ge(cur1_summed, 2 * b + 2)
                    if not (isinstance(b, int) and b == 0):
                        dve.wait_ge(m1_done, b)
                    nc.vector.tensor_tensor(feat_a[:, :], csum[:, 0, :], csum[:, 1, :],
                                            ALU.add).then_inc(feat_a_ready, 1)

            dve.wait_ge(w0_in, 32)
            nc.vector.tensor_tensor(w0_sb[:, :, :], w0_sb[:, :, :], w0b_sb, ALU.add).then_inc(w0_ready, 1)
            dve.wait_ge(w0_ready, 1)
            dve.wait_ge(w1_in, 16)
            for k in range(len(EITHER)):
                nc.vector.tensor_copy(w1_high[:, k, :], w1s_sb[:, k, :]).then_inc(w1_high_ready, 1)
            dve.wait_ge(w1_high_ready, len(EITHER))
            for k in range(len(EITHER)):
                nc.vector.tensor_tensor(w1_low[:, k, :], w1s_sb[:, k, :],
                                        w1_high[:, k, :].bitcast(fp32),
                                        ALU.subtract).then_inc(w1_low_ready, 1)
            dve.wait_ge(w1_low_ready, len(EITHER))
            layer0(0, 0, 0, 0)
            layer0(0, 1, N0, N0)
            sum_direct(0, 0)

            def body(b, more_h, first=False):
                n = FIRST + PER_BLOCK * b
                slot = FIRST
                for p in range(2):
                    def sums():
                        if p == 0:
                            sum_direct(b, 1)
                            if not first:
                                sum_cur1(b - 1, 1)
                        else:
                            join_direct(b)
                            if more_h:
                                dve.wait_ge(feat_b_ready, b + 1)
                                sum_direct(b + 1, 0)
                            sum_cur1(b, 0)

                    layer1(b, p, n, slot, NSPLIT * b + SPLIT_AT[p], sums)
                    n, slot = n + N1, slot + N1
                    if more_h:
                        layer0(b + 1, p, n, slot)
                        n, slot = n + N0, slot + N0

            body(0, True, True)
            body(1, True)
            with dve.Fori(2, BLOCKS - 1) as b:
                body(b, True)
            body(BLOCKS - 1, False)
            sum_cur1(BLOCKS - 1, 1)

        @block.tensor
        def _(pe):
            def transpose(b):
                pe.wait_ge(gathered, GATH_SEM * (b + 1))
                if not (isinstance(b, int) and b == 0):
                    pe.wait_ge(emb_t_ready, b)
                for c in range(TCH):
                    m = PART if c < TCH - 1 else TLAST
                    last = nc.tensor.transpose(ps_t[0:m, c // 4, c % 4 * PART:(c % 4 + 1) * PART],
                                               emb[:, c * PART:c * PART + m], ident_sb[:, :])
                last.then_inc(transposed, 1)

            def layer0(b, p, n, slot, first=False):
                if not first:
                    pe.wait_ge(cur0_ready, 2 * b + p)
                for c in range(N0):
                    pe.wait_ge(made, n + c + 1)
                    for half in range(COLS // BANK):
                        cols = slice(half * BANK, (half + 1) * BANK)
                        last = nc.tensor.matmul(acc0[:, cols], w0_sb[:, c, :],
                                                prod[0:K0, (slot + c) % RING, cols],
                                                start=(c == 0), stop=(c == N0 - 1))
                    last.then_inc(used, 1)

            def layer1(b, p, n, slot, splits, first=False, inside=None):
                if not first:
                    pe.wait_ge(cur1_ready, 2 * b + p)
                for c in range(N1):
                    if c in SPLIT[p]:
                        k = SPLIT[p].index(c)
                        at, w = SPLIT_AT[p] + k, EITHER.index(c)
                        pe.wait_ge(high_made, splits + k + 1)
                        passes = [(w1_high, high[:, at % HIGHS]), (w1_low, high[:, at % HIGHS]),
                                  (w1_high, low[:, at % LOWS])]
                        for i, (weights, values) in enumerate(passes):
                            if i == 2:
                                pe.wait_ge(low_made, splits + k + 1)
                            for half in range(COLS // BANK):
                                cols = slice(half * BANK, (half + 1) * BANK)
                                last = nc.tensor.matmul(acc1[:, cols], weights[:, w, :],
                                                        values[:, cols],
                                                        start=False, stop=False)
                    else:
                        pe.wait_ge(made, n + c + 1)
                        for half in range(COLS // BANK):
                            cols = slice(half * BANK, (half + 1) * BANK)
                            last = nc.tensor.matmul(acc1[:, cols], w1_sb[:, WHOLE.index(c), :],
                                                    prod[:, (slot + c) % RING, cols],
                                                    start=(c == 0), stop=(c == N1 - 1))
                    last.then_inc(used, 1)
                    if inside and c == MID:
                        inside()

            def mlp1(b):
                pe.wait_ge(feat_a_ready, b + 1)
                pe.wait_ge(feat_b_ready, b + 1)
                pe.wait_ge(context_in, 16 * (b + 1))
                if not (isinstance(b, int) and b == 0):
                    pe.wait_ge(hid1_ready, b)
                for m in range(M1):
                    cols = slice(m * PART, (m + 1) * PART)
                    nc.tensor.matmul(ps_m1[:, m, :], wt1a_sb[:, cols], feat_a[:, :],
                                     start=True, stop=False)
                    last = nc.tensor.matmul(ps_m1[:, m, :], wt1b_sb[:, cols],
                                            feat_b[:, :],
                                            start=False, stop=True)
                last.then_inc(m1_done, 1)

            def mlp2(b):
                pe.wait_ge(hid1_ready, b + 1)
                if not (isinstance(b, int) and b == 0):
                    pe.wait_ge(y_ready, b)
                for m in range(M2):
                    for k in range(M1):
                        last = nc.tensor.matmul(ps_m2[:, m * PART:(m + 1) * PART],
                                                wt2_sb[:, k, m * PART:(m + 1) * PART],
                                                hid1[:, k, :], start=(k == 0), stop=(k == M1 - 1))
                last.then_inc(m2_done, 1)

            def mlp3(b):
                pe.wait_ge(hid2_ready, b + 1)
                for k in range(M2):
                    last = nc.tensor.matmul(ps_m2[0:1, 3 * PART:], wt3_sb[:, k:k + 1], hid2[:, k, :],
                                            start=(k == 0), stop=(k == M2 - 1))
                last.then_inc(m3_done, 1)

            pe.wait_ge(weights_in, 16 * 8)
            transpose(0)
            pe.wait_ge(w0_ready, 1)
            layer0(0, 0, 0, 0, True)
            layer0(0, 1, N0, N0)
            transpose(1)
            pe.wait_ge(w1_low_ready, len(EITHER))

            def body(b, more_x, more_h, mlp, first=False):
                n = FIRST + PER_BLOCK * b
                slot = FIRST
                for p in range(2):
                    layer1(b, p, n, slot, NSPLIT * b + SPLIT_AT[p], first and p == 0,
                           (lambda: mlp2(b - 1)) if p and mlp else None)
                    n, slot = n + N1, slot + N1
                    if p and mlp:
                        mlp3(b - 1)
                    if more_h:
                        layer0(b + 1, p, n, slot)
                        n, slot = n + N0, slot + N0
                    if p == 0:
                        if more_x:
                            transpose(b + 2)
                        if mlp:
                            mlp1(b - 1)

            body(0, True, True, False, True)
            body(1, True, True, True)
            with pe.Fori(2, BLOCKS - 2) as b:
                body(b, True, True, True)
            body(BLOCKS - 2, False, True, True)
            body(BLOCKS - 1, False, False, True)
            mlp1(BLOCKS - 1)
            mlp2(BLOCKS - 1)
            mlp3(BLOCKS - 1)


def w0_rows():
    import numpy as np
    first = np.full((K0, N0), -1)
    second = np.full((K0, N0), -1)
    seen = set()
    for c, (t, u) in enumerate(PAIRS0):
        for q in range(3):
            for r in range(FIELDS):
                i, j = (r + SHIFTS[t][q]) % FIELDS, (r + SHIFTS[u][q]) % FIELDS
                if (min(i, j), max(i, j)) in seen:
                    continue
                seen.add((min(i, j), max(i, j)))
                first[q * FIELDS + r, c] = i * FIELDS + j
                if i != j:
                    second[q * FIELDS + r, c] = j * FIELDS + i
    assert len(seen) == FIELDS * (FIELDS + 1) // 2
    return first, second


def kernel(**inputs):
    import numpy as np
    import concourse.bacc as bacc
    from concourse.bass_utils import run_bass_kernel_spmd

    def rows_of(w, at):
        padded = np.concatenate([w, np.zeros((1, w.shape[1]), w.dtype)])
        return np.ascontiguousarray(padded[at])

    a = {k: np.asarray(v) for k, v in inputs.items()}
    ids = np.ascontiguousarray(a["ids"].reshape(BLOCKS, PART, FIELDS).transpose(1, 0, 2)).reshape(PART, -1).view(np.uint32)
    w0 = np.concatenate([a["L0_rec_W0"][:, HALF:], a["L0_rec_W0"][:, :HALF]], axis=1)
    first, second = w0_rows()
    r = np.arange(PART)
    w1_at = np.stack([np.where(8 * t + r % 8 < FIELDS, (8 * t + r % 8) * HALF + 16 * u + r // 8, -1)
                      for t, u in PAIRS1], axis=1)
    wt1 = a["W_top1"]
    arrays = {
        "ids": ids,
        "ctx_t": np.ascontiguousarray(a["dense_ctx"].T),
        "w0a": rows_of(w0, first),
        "w0b": rows_of(w0, second),
        "w1": rows_of(a["L0_rec_W1"], w1_at[:, WHOLE]),
        "w1s": rows_of(a["L0_rec_W1"], w1_at[:, EITHER]),
        "b1": np.ascontiguousarray(a["b_top1"].reshape(M1, PART).T),
        "b2": np.ascontiguousarray(a["b_top2"].reshape(M2, PART).T),
        "wt1a": np.ascontiguousarray(wt1[HALF:HALF + CH]),
        "wt1b": np.concatenate([wt1[:HALF], wt1[HALF + CH:]]),
        "wt2": np.ascontiguousarray(a["W_top2"].reshape(M1, PART, H2).transpose(1, 0, 2)),
        "wt3": np.ascontiguousarray(a["W_top3"].reshape(M2, PART).T),
        "ident": np.eye(PART, dtype=np.float32),
    }
    nc = bacc.Bacc("TRN2", target_bir_lowering=False, num_devices=1)
    fed, aps = {}, {}
    for name, x in list(arrays.items()) + [(f"tbl_{f}", a[f"tbl_{f}"]) for f in range(FIELDS)]:
        fed[f"in_{name}"] = x
        aps[name] = nc.dram_tensor(f"in_{name}", x.shape, mybir.dt.from_np(x.dtype), kind="ExternalInput").ap()
    out = nc.dram_tensor("out_y", (1, BATCH), mybir.dt.float32, kind="ExternalOutput").ap()
    tables = [aps.pop(f"tbl_{f}") for f in range(FIELDS)]
    cin_kernel(nc, tables=tables, out=out, **aps)
    got = run_bass_kernel_spmd(nc, [fed], core_ids=[0])
    return got.results[0]["out_y"].reshape(BATCH, 1)
```

```python
import concourse.bass as bass
from concourse import mybir
from contextlib import ExitStack

BATCH, FIELDS, DIM, CH, HALF = 2048, 39, 16, 128, 64
PART = 128
BLOCKS = BATCH // PART
BLOCK_COLS = PART * DIM
COLS = BLOCK_COLS // 2
DIMS = DIM // 2
BANK = 512
XROWS = 2 * FIELDS

X_BLOCK = XROWS * BLOCK_COLS

SHIFTS = [[34, 14, 30], [8, 5, 1], [15, 28, 30], [11, 0, 9], [33, 2, 24]]
PAIRS0 = [(0, 1), (1, 2), (2, 3), (3, 4), (0, 2), (1, 3), (4, 0)]
K0 = 3 * FIELDS
XT, HT = 5, 4
PAIRS1 = [(t, u) for u in range(HT) for t in range(XT)]
N0, N1 = len(PAIRS0), len(PAIRS1)
L0, L1_EVEN, L1_ODD = 0, 1, 2
COUNT = [N0, N1, N1]

RING = 9
SPLIT = [[1, 3, 4], [2, 7, 9, 12, 14, 16, 18], [2, 4, 7, 9, 12, 14, 16, 18]]
EITHER = sorted(set(SPLIT[L1_EVEN] + SPLIT[L1_ODD]))
WHOLE = [c for c in range(N1) if c not in SPLIT[L1_EVEN] or c not in SPLIT[L1_ODD]]
HIGHS, LOWS = 3, 3
LAG = 2
GROUP = 2
AHEAD = 5
SUM_CUR1, MLP1, SUM_DIRECT, JOIN_DIRECT = 4, 7, 13, 18
MLP2, NEW_X = 9, 14
NEXT_X = 7


def phases(layers, n, k):
    out = []
    for layer in layers:
        out.append((layer, n, k))
        n, k = n + COUNT[layer], k + len(SPLIT[layer])
    return out, n, k


PROLOGUE, N_FIRST, K_FIRST = phases([L0, L0], 0, 0)
BLOCK, n_end, k_end = phases([L1_EVEN, L0, L1_ODD, L0], N_FIRST, K_FIRST)
N_BLOCK, K_BLOCK = n_end - N_FIRST, k_end - K_FIRST
LAST = phases([L1_EVEN, L1_ODD], N_FIRST, K_FIRST)[0]
assert N_BLOCK % RING == 0 and K_BLOCK % HIGHS == K_BLOCK % LOWS == 0


def begins(phase, b):
    _, n, k = phase
    return n + N_BLOCK * b, k + K_BLOCK * b, n % RING, k % (HIGHS * LOWS)


def distance(phase, b, i, slots):
    if isinstance(b, int) and b == 0:
        some, k = PROLOGUE + BLOCK, phase[2] + i
    else:
        some, k = BLOCK + [(layer, n + N_BLOCK, k + K_BLOCK) for layer, n, k in
                           (LAST if phase in LAST[1:] else BLOCK)], phase[2] + i + K_BLOCK
    at = {first + j: n + c for layer, n, first in some for j, c in enumerate(SPLIT[layer])}
    return at[k] - at[k - slots] if k >= slots else 0


def groups(pairs, slot, most):
    out = []
    for c, (t, u) in enumerate(pairs):
        neighbours = c and pairs[c - 1] == ((t - 1, u - 1) if pairs is PAIRS0 else (t - 1, u))
        if neighbours and len(out[-1]) < most and (slot + c) % RING:
            out[-1].append(c)
        else:
            out.append([c])
    return out


TCH = 5
TLAST = FIELDS * DIM - 4 * PART
H1, H2, CTX = 512, 256, 16
M1, M2 = H1 // PART, H2 // PART
KB = HALF + CTX


def cin_kernel(nc, ids, tables, ctx_t, w0a, w0b, w1, w1s, b1, b2, wt1a, wt1b, wt2, wt3, ident, out):
    fp32, fp32r, u32 = mybir.dt.float32, mybir.dt.float32r, mybir.dt.uint32
    ALU, ACT, AX = mybir.AluOpType, mybir.ActivationFunctionType, mybir.AxisListType

    with ExitStack() as ctx:
        def sb(name, shape, dt=fp32):
            return ctx.enter_context(nc.sbuf_tensor(name, shape, dt))

        def ps(name, shape):
            return ctx.enter_context(nc.psum_tensor(name, shape, fp32))

        def sem(name):
            return ctx.enter_context(nc.semaphore(name))

        x_dram = nc.dram_tensor("x_dram", [BLOCKS * XROWS * BLOCK_COLS], fp32, kind="Internal").ap()
        h_dram = nc.dram_tensor("h_dram", [2, HALF, COLS], fp32, kind="Internal").ap()

        ids_now = sb("ids_now", [PART, FIELDS], u32)
        emb = sb("emb", [PART, FIELDS * DIM])
        emb_t = sb("emb_t", [PART, TCH * PART])
        ident_sb = sb("ident_sb", [PART, PART])
        shift_x = sb("shift_x", [PART, len(SHIFTS), COLS])
        tile_x = sb("tile_x", [PART, 2, XT, COLS])
        tile_h = sb("tile_h", [PART, 2, HT, COLS])
        prod = sb("prod", [PART, RING, COLS])
        high = sb("high", [PART, HIGHS, COLS], fp32r)
        low = sb("low", [PART, LOWS, COLS], fp32r)
        direct = sb("direct", [PART, COLS])
        next_h = sb("next_h", [PART, COLS])
        dsum = sb("dsum", [PART, PART])
        cur1 = sb("cur1", [PART, 2, COLS])
        w0_sb = sb("w0_sb", [K0, N0, CH])
        w1_sb = sb("w1_sb", [PART, len(WHOLE), CH])
        w0_high = sb("w0_high", [K0, len(SPLIT[L0]), CH], fp32r)
        w0_low = sb("w0_low", [K0, len(SPLIT[L0]), CH], fp32r)
        w1_high = sb("w1_high", [PART, len(EITHER), CH], fp32r)
        w1_low = sb("w1_low", [PART, len(EITHER), CH], fp32r)
        feat_a = sb("feat_a", [PART, PART])
        feat_b = sb("feat_b", [KB, PART])
        wt1a_sb = sb("wt1a_sb", [PART, H1])
        wt1b_sb = sb("wt1b_sb", [KB, H1])
        wt2_sb = sb("wt2_sb", [PART, M1, H2])
        wt3_sb = sb("wt3_sb", [PART, M2])
        b1_sb = sb("b1_sb", [PART, M1])
        b2_sb = sb("b2_sb", [PART, M2])
        hid1 = sb("hid1", [PART, M1, PART])
        hid2 = sb("hid2", [PART, M2, PART])
        small = sb("small", [PART, PART])
        dsum_odd = small[0:HALF, :]
        y_now = small[HALF:HALF + 1, :]
        w0b_sb = prod[0:K0, 0, 0:N0 * CH].rearrange("p (c l) -> p c l", c=N0)
        w1s_sb = prod[:, 1:3, :].rearrange("p a (c l) -> p (a c) l", l=CH)[:, 0:len(EITHER), :]

        acc0 = ps("acc0", [PART, COLS])
        acc1 = ps("acc1", [PART, COLS])
        ps_t = ps("ps_t", [PART, 2, BANK])
        ps_m1 = ps("ps_m1", [PART, M1, PART])
        ps_m2 = ps("ps_m2", [PART, BANK])

        ids_in = sem("ids_in")
        first_ids_in = sem("first_ids_in")
        gathers_begun = sem("gathers_begun")
        gathered = sem("gathered")
        first_rows = [sem(f"first_rows_{c}") for c in range(TCH)]
        weights_in = sem("weights_in")
        w0_in = sem("w0_in")
        w0_ready = sem("w0_ready")
        transposed = sem("transposed")
        emb_t_ready = sem("emb_t_ready")
        first_transposed = sem("first_transposed")
        first_emb_t = sem("first_emb_t")
        x_stored = sem("x_stored")
        first_shift = [sem(f"first_shift_{t}") for t in range(len(SHIFTS))]
        shift_loaded = sem("shift_loaded")
        shift_loaded_1 = sem("shift_loaded_1")
        x_tiles_loaded = [sem("x_tiles_loaded_even"), sem("x_tiles_loaded_odd")]
        h_tiles_loaded = [sem("h_tiles_loaded_even"), sem("h_tiles_loaded_odd")]
        first_h = [sem(f"first_h_{u}") for u in range(HT)]
        h_stored = [sem("h_stored_even"), sem("h_stored_odd")]
        made = sem("made")
        used = sem("used")
        high_made = sem("high_made")
        low_made = sem("low_made")
        w1_in = sem("w1_in")
        context_in = sem("context_in")
        weights_high = sem("weights_high")
        weights_low = sem("weights_low")
        next_h_ready = sem("next_h_ready")
        cur0_ready = sem("cur0_ready")
        direct_summed = sem("direct_summed")
        dsum_odd_ready = sem("dsum_odd_ready")
        cur1_ready = sem("cur1_ready")
        feat_b_ready = sem("feat_b_ready")
        feat_a_ready = sem("feat_a_ready")
        m1_done = sem("m1_done")
        m2_done = sem("m2_done")
        m3_done = sem("m3_done")
        hid1_ready = sem("hid1_ready")
        hid2_ready = sem("hid2_ready")
        y_ready = sem("y_ready")
        y_stored = sem("y_stored")

        SHIFT_SEM = 16 * 3 * len(SHIFTS)
        X_SEM, H_SEM = 16 * XT, 16 * HT
        XST_SEM, FIRST_XST = 16 * 4, 16 * 2 * TCH
        GATH_SEM = 16 * FIELDS

        block = ctx.enter_context(nc.Block())

        @block.sync
        def _(sp):
            def load_shift(x_at, p, to=shift_x, signals=[shift_loaded] * len(SHIFTS)):
                base = x_at + p * COLS
                for t, shifts in enumerate(SHIFTS):
                    for q, a in enumerate(shifts):
                        src = bass.AP(x_dram.tensor, base + a * BLOCK_COLS,
                                      [[BLOCK_COLS, FIELDS], [1, COLS]])
                        sp.dma_start(to[q * FIELDS:(q + 1) * FIELDS, t, :],
                                     src).then_inc(signals[t], 16)

            def load_x(x_at, p):
                base = x_at + p * COLS
                for t in range(XT):
                    src = bass.AP(x_dram.tensor, base + t * 8 * BLOCK_COLS,
                                  [[0, 16], [BLOCK_COLS, 8], [1, COLS]])
                    sp.dma_start(tile_x[:, p, t, :], src).then_inc(x_tiles_loaded[p], 16)

            def load_h(p, signals=None):
                for u in range(HT):
                    src = bass.AP(h_dram.tensor, p * HALF * COLS + u * 16 * COLS,
                                  [[COLS, 16], [0, 8], [1, COLS]])
                    sp.dma_start(tile_h[:, p, u, :], src
                                 ).then_inc(signals[u] if signals else h_tiles_loaded[p], 16)

            def store_x(x_at, blocks):
                sp.wait_ge(emb_t_ready, blocks)
                for copy in range(2):
                    base = x_at + copy * FIELDS * BLOCK_COLS
                    full = bass.AP(x_dram.tensor, base, [[PART, PART], [PART * PART, 4], [1, PART]])
                    rest = bass.AP(x_dram.tensor, base + 4 * PART * PART, [[PART, TLAST], [1, PART]])
                    sp.dma_start(full, emb_t[:, 0:4 * PART].rearrange("p (c b) -> p c b", c=4)
                                 ).then_inc(x_stored, 16)
                    sp.dma_start(rest, emb_t[0:TLAST, 4 * PART:]).then_inc(x_stored, 16)

            def store_first_x():
                for c in range(TCH):
                    m = PART if c < TCH - 1 else TLAST
                    sp.wait_ge(first_emb_t, c + 1)
                    for copy in range(2):
                        to = bass.AP(x_dram.tensor, copy * FIELDS * BLOCK_COLS + c * PART * PART,
                                     [[PART, m], [1, PART]])
                        sp.dma_start(to, emb_t[0:m, c * PART:(c + 1) * PART]).then_inc(x_stored, 16)

            def load_context(at, blocks):
                if not isinstance(blocks, int) or blocks:
                    sp.wait_ge(m1_done, blocks)
                sp.dma_start(feat_b[HALF:, :], ctx_t[:, bass.ds(at, PART)]).then_inc(context_in, 16)

            def store_h(p, steps):
                sp.wait_ge(next_h_ready, steps)
                half = slice(HALF, PART) if p == 0 else slice(0, HALF)
                sp.dma_start(h_dram[p], next_h[half, :]).then_inc(h_stored[p], 16)

            sp.dma_start(ids_now[:, :], ids[:, 0:FIELDS]).then_inc(first_ids_in, 16)
            sp.dma_start(ident_sb[:, :], ident).then_inc(weights_in, 16)
            sp.dma_start(w0_sb[:, :, :], w0a).then_inc(w0_in, 16)
            sp.dma_start(w0b_sb, w0b).then_inc(w0_in, 16)
            sp.dma_start(w1s_sb, w1s).then_inc(w1_in, 16)
            sp.dma_start(w1_sb[:, :, :], w1).then_inc(weights_in, 16)
            sp.dma_start(wt1a_sb[:, :], wt1a).then_inc(weights_in, 16)
            sp.dma_start(wt1b_sb[:, :], wt1b).then_inc(weights_in, 16)
            sp.dma_start(wt2_sb[:, :, :], wt2).then_inc(weights_in, 16)
            sp.dma_start(wt3_sb[:, :], wt3).then_inc(weights_in, 16)
            sp.dma_start(b1_sb[:, :], b1).then_inc(weights_in, 16)
            sp.dma_start(b2_sb[:, :], b2).then_inc(weights_in, 16)

            store_first_x()
            sp.wait_ge(x_stored, FIRST_XST)
            load_shift(0, 0, shift_x, first_shift)
            load_shift(0, 1, tile_x[:, 1], [shift_loaded_1] * len(SHIFTS))
            load_x(0, 0)
            store_h(0, 1)
            sp.wait_ge(h_stored[0], 16)
            load_h(0, first_h)

            def body(b, more_x, more_h, x_is_stored=True):
                value = (lambda v: v if isinstance(v, int) else sp.snap(v))
                x_now, x_next = value(b * X_BLOCK), value((b + 1) * X_BLOCK)
                x_after = value((b + 2) * X_BLOCK)
                stores_odd, stores_even = value(16 * (b + 1)), value(16 * (b + 2))
                relus_odd, relus_even = value(2 * b + 2), value(2 * b + 3)
                relu1s_odd, relu1s_even = value(2 * b), value(2 * b + 1)
                emb_blocks, x_stores = value(b + 2), value(FIRST_XST + XST_SEM * (b + 2))
                context_at = value(b * PART)

                if x_is_stored:
                    sp.wait_ge(cur1_ready, relu1s_odd)
                    load_x(x_now, 1)
                store_h(1, relus_odd)
                if more_h and x_is_stored:
                    load_shift(x_next, 0)
                sp.wait_ge(h_stored[1], stores_odd)
                load_h(1)
                if not x_is_stored:
                    store_x(X_BLOCK, 1)
                    sp.wait_ge(x_stored, FIRST_XST + XST_SEM)
                    load_shift(X_BLOCK, 0)
                    load_x(0, 1)
                if more_h:
                    sp.wait_ge(cur1_ready, relu1s_even)
                    load_x(x_next, 0)
                    store_h(0, relus_even)
                    load_shift(x_next, 1)
                    sp.wait_ge(h_stored[0], stores_even)
                    load_h(0)
                if more_x:
                    store_x(x_after, emb_blocks)
                    sp.wait_ge(x_stored, x_stores)
                load_context(context_at, b)

            body(0, True, True, False)
            with sp.Fori(1, BLOCKS - 2) as b:
                body(b, True, True)
            body(BLOCKS - 2, False, True)
            body(BLOCKS - 1, False, False)

        @block.gpsimd
        def _(pool):
            def gather(b, rows_in):
                if isinstance(b, int) and b == 0:
                    pool.wait_ge(first_ids_in, 16)
                else:
                    pool.wait_ge(ids_in, 16 * b)
                pool.sem_inc(gathers_begun, 1)
                for f in range(FIELDS):
                    nc.gpsimd.indirect_dma_start(
                        out=emb[:, f * DIM:(f + 1) * DIM], out_offset=None, in_=tables[f],
                        in_offset=bass.IndirectOffsetOnAxis(ap=ids_now[:, f:f + 1], axis=0),
                    ).then_inc(rows_in(f), 16)

            def load_ids(b):
                pool.dma_start(ids_now[:, :], ids[:, bass.ds(b * FIELDS, FIELDS)]).then_inc(ids_in, 16)

            gather(0, lambda f: first_rows[f // 8])
            for c in range(TCH):
                pool.wait_ge(first_rows[c], 16 * min(8, FIELDS - 8 * c))
            load_ids(1)
            pool.wait_ge(first_transposed, TCH)
            gather(1, lambda f: gathered)
            with pool.Fori(2, BLOCKS) as b:
                pool.wait_ge(gathered, GATH_SEM * (b - 1))
                load_ids(b)
                pool.wait_ge(transposed, b - 1)
                gather(b, lambda f: gathered)

        @block.scalar
        def _(act):
            def relu0(b, p, l0_end, first=False):
                act.wait_ge(used, l0_end)
                if not first:
                    act.wait_ge(direct_summed, b)
                    act.wait_ge(h_stored[p], 16 * b)
                upper, lower = slice(0, HALF), slice(HALF, PART)
                nc.scalar.activation(next_h[lower if p == 0 else upper, :], acc0[HALF:, :],
                                     ACT.Relu).then_inc(next_h_ready, 1)
                nc.scalar.activation(direct[upper if p == 0 else lower, :], acc0[0:HALF, :],
                                     ACT.Relu).then_inc(cur0_ready, 1)

            def move_dsum(b):
                act.wait_ge(direct_summed, b + 1)
                nc.scalar.activation(dsum_odd, dsum[HALF:, :], ACT.Copy).then_inc(dsum_odd_ready, 1)

            def relu1(b, p, l1_end, first=False):
                act.wait_ge(used, l1_end)
                if not first:
                    act.wait_ge(feat_a_ready, b)
                nc.scalar.activation(cur1[:, p, :], acc1[:, :], ACT.Relu).then_inc(cur1_ready, 1)

            def evacuate_first():
                for c in range(TCH):
                    m = PART if c < TCH - 1 else TLAST
                    act.wait_ge(first_transposed, c + 1)
                    nc.scalar.activation(emb_t[0:m, c * PART:(c + 1) * PART],
                                         ps_t[0:m, c % 2, c // 2 * PART:(c // 2 + 1) * PART],
                                         ACT.Copy).then_inc(first_emb_t, 1)

            def evacuate(b):
                act.wait_ge(transposed, b)
                act.wait_ge(x_stored, FIRST_XST + XST_SEM * (b - 1))
                nc.scalar.activation(emb_t[:, 0:4 * PART], ps_t[:, 0, :], ACT.Copy)
                nc.scalar.activation(emb_t[0:TLAST, 4 * PART:], ps_t[0:TLAST, 1, 0:PART],
                                     ACT.Copy).then_inc(emb_t_ready, 1)

            def hidden1(b):
                act.wait_ge(m1_done, b + 1)
                for m in range(M1):
                    last = nc.scalar.activation(hid1[:, m, :], ps_m1[:, m, :], ACT.Relu,
                                                bias=b1_sb[:, m:m + 1])
                last.then_inc(hid1_ready, 1)

            def hidden2(b):
                act.wait_ge(m2_done, b + 1)
                for m in range(M2):
                    last = nc.scalar.activation(hid2[:, m, :], ps_m2[:, m * PART:(m + 1) * PART],
                                                ACT.Relu, bias=b2_sb[:, m:m + 1])
                last.then_inc(hid2_ready, 1)

            def score(b):
                act.wait_ge(m3_done, b + 1)
                if not (isinstance(b, int) and b == 0):
                    act.wait_ge(y_stored, 16 * b)
                nc.scalar.activation(y_now[:, :], ps_m2[0:1, 3 * PART:],
                                     ACT.Copy).then_inc(y_ready, 1)
                act.wait_ge(y_ready, b + 1)
                act.dma_start(out[:, bass.ds(b * PART, PART)], y_now[:, :]).then_inc(y_stored, 16)

            def round_high(phase, b, rows=PART, only=None):
                n, k, slot, part = begins(phase, b)
                for i, c in enumerate(SPLIT[phase[0]]):
                    if only is not None and c not in only:
                        continue
                    act.wait_ge(made, n + c + 1)
                    away = distance(phase, b, i, HIGHS)
                    if 0 < away < RING:
                        act.wait_ge(used, n + c + 1 - away)
                    nc.scalar.activation(high[0:rows, (part + i) % HIGHS, :],
                                         prod[0:rows, (slot + c) % RING, :],
                                         ACT.Copy).then_inc(high_made, 1)

            early = range(AHEAD)
            evacuate_first()
            round_high(PROLOGUE[0], 0, K0)
            round_high(PROLOGUE[1], 0, K0, range(2))
            relu0(0, 0, N0, True)
            round_high(PROLOGUE[1], 0, K0, range(2, N0))
            act.wait_ge(weights_in, 16 * 8)

            def body(b, more_x, more_h, mlp, first=False):
                even, odd = (BLOCK[0], BLOCK[2]) if more_h else LAST
                round_high(even, b, only=early)
                relu0(b, 1, begins(even, b)[0], first)
                if mlp:
                    round_high(even, b, only=range(AHEAD, JOIN_DIRECT - 1))
                    hidden1(b - 1)
                else:
                    round_high(even, b, only=range(AHEAD, NEXT_X + AHEAD + 1))
                    evacuate(1)
                    round_high(even, b, only=range(NEXT_X + AHEAD + 1, JOIN_DIRECT - 1))
                move_dsum(b)
                round_high(even, b, only=range(JOIN_DIRECT - 1, N1))
                if more_h:
                    round_high(BLOCK[1], b, K0)
                relu1(b, 0, begins(even, b)[0] + N1, first)
                round_high(odd, b, only=early)
                if more_h:
                    relu0(b + 1, 0, begins(odd, b)[0])
                round_high(odd, b, only=range(AHEAD, MLP2 + AHEAD + 1))
                if mlp:
                    hidden2(b - 1)
                round_high(odd, b, only=range(MLP2 + AHEAD + 1, NEW_X + AHEAD + 1))
                if more_x:
                    evacuate(b + 2)
                round_high(odd, b, only=range(NEW_X + AHEAD + 1, N1))
                if more_h:
                    round_high(BLOCK[3], b, K0)
                relu1(b, 1, begins(odd, b)[0] + N1, first)
                if mlp:
                    score(b - 1)

            body(0, True, True, False, True)
            body(1, True, True, True)
            with act.Fori(2, BLOCKS - 2) as b:
                body(b, True, True, True)
            body(BLOCKS - 2, False, True, True)
            body(BLOCKS - 1, False, False, True)
            hidden1(BLOCKS - 1)
            hidden2(BLOCKS - 1)
            score(BLOCKS - 1)
            act.wait_ge(y_stored, 16 * BLOCKS)

        @block.vector
        def _(dve):
            def multiply(n, slot, group, a, b, rows):
                many = len(group)
                if not (isinstance(n, int) and n + many <= RING):
                    dve.wait_ge(used, n + many - RING)
                nc.vector.tensor_tensor(prod[0:rows, slot:slot + many, :], a, b,
                                        ALU.mult).then_inc(made, many)

            def subtract(phase, b, i, c, newest, rows):
                n, k, slot, part = begins(phase, b)
                dve.wait_ge(high_made, k + i + 1)
                away = distance(phase, b, i, LOWS)
                if away and c - away > newest - RING:
                    dve.wait_ge(used, n + c + 1 - away)
                nc.vector.tensor_tensor(low[0:rows, (part + i) % LOWS, :],
                                        prod[0:rows, (slot + c) % RING, :],
                                        high[0:rows, (part + i) % HIGHS, :].bitcast(fp32),
                                        ALU.subtract).then_inc(low_made, 1)

            def layer(phase, b, pairs, operands, rows, before={}, behind={}, most=GROUP):
                n, k, slot, part = begins(phase, b)
                made_here, waiting = 0, list(enumerate(SPLIT[phase[0]]))
                for group in groups(pairs, slot, most):
                    for c in group:
                        if c in before:
                            before[c]()
                    multiply(n + made_here, (slot + made_here) % RING, group, *operands(group), rows)
                    made_here += len(group)
                    while waiting and (made_here > waiting[0][1] + LAG or made_here == len(pairs)):
                        i, c = waiting.pop(0)
                        subtract(phase, b, i, c, made_here - 1, rows)
                    for c in group:
                        if c in behind:
                            behind[c]()

            def layer0(phase, b, tiles, before={}, most=GROUP):
                def operands(group):
                    (t, u), many = PAIRS0[group[0]], len(group)
                    return tiles[0:K0, t:t + many, :], tiles[0:K0, u:u + many, :]

                layer(phase, b, PAIRS0, operands, K0, before, most=most)

            def layer1(phase, b, p, before={}, behind={}):
                def operands(group):
                    (t, u), many = PAIRS1[group[0]], len(group)
                    h = tile_h[:, p, u:u + 1, :]
                    return tile_x[:, p, t:t + many, :], h.broadcast_to([PART, many, COLS]) if many > 1 else h

                dve.wait_ge(x_tiles_loaded[p], X_SEM * (b + 1))
                layer(phase, b, PAIRS1, operands, PART, before, behind)

            def sum_direct(b):
                dve.wait_ge(cur0_ready, 2 * b + 2)
                nc.vector.tensor_reduce(dsum[:, :], direct[:, :].rearrange("l (d b) -> l b d", d=DIMS),
                                        AX.X, ALU.add).then_inc(direct_summed, 1)

            def join_direct(b):
                dve.wait_ge(dsum_odd_ready, b + 1)
                if not (isinstance(b, int) and b == 0):
                    dve.wait_ge(m1_done, b)
                nc.vector.tensor_tensor(feat_b[0:HALF, :], dsum[0:HALF, :], dsum_odd,
                                        ALU.add).then_inc(feat_b_ready, 1)

            def sum_cur1(b):
                dve.wait_ge(cur1_ready, 2 * b + 2)
                if not (isinstance(b, int) and b == 0):
                    dve.wait_ge(m1_done, b)
                nc.vector.tensor_reduce(
                    feat_a[:, :], cur1[:, :, :].rearrange("l p (d b) -> l b (p d)", d=DIMS),
                    AX.X, ALU.add).then_inc(feat_a_ready, 1)

            dve.wait_ge(w0_in, 32)
            nc.vector.tensor_tensor(w0_sb[:, :, :], w0_sb[:, :, :], w0b_sb, ALU.add).then_inc(w0_ready, 1)
            dve.wait_ge(w0_ready, 1)
            dve.wait_ge(w1_in, 16)
            split_weights = [(w0_sb[:, c, :], w0_high[:, i, :], w0_low[:, i, :])
                             for i, c in enumerate(SPLIT[L0])]
            split_weights += [(w1s_sb[:, i, :], w1_high[:, i, :], w1_low[:, i, :])
                              for i in range(len(EITHER))]
            for weights, w_high, _ in split_weights:
                nc.vector.tensor_copy(w_high, weights).then_inc(weights_high, 1)
            dve.wait_ge(weights_high, len(split_weights))
            for weights, w_high, w_low in split_weights:
                nc.vector.tensor_tensor(w_low, weights, w_high.bitcast(fp32),
                                        ALU.subtract).then_inc(weights_low, 1)
            dve.wait_ge(weights_low, len(split_weights))
            dve.wait_ge(first_shift[0], 16 * 3)
            newest = {}
            for c, tiles in enumerate(PAIRS0):
                newest.setdefault(max(tiles), c)
            layer0(PROLOGUE[0], 0, shift_x,
                   {c: lambda t=t: dve.wait_ge(first_shift[t], 16 * 3) for t, c in newest.items()}, most=1)
            dve.wait_ge(shift_loaded_1, SHIFT_SEM)
            layer0(PROLOGUE[1], 0, tile_x[:, 1])

            def body(b, more_h, first=False):
                steps = (BLOCK[0], BLOCK[2]) if more_h else LAST
                for p in range(2):
                    behind = {}
                    if p == 0:
                        behind[SUM_DIRECT] = lambda: sum_direct(b)
                        behind[JOIN_DIRECT] = lambda: join_direct(b)
                        if not first:
                            behind[SUM_CUR1] = lambda: sum_cur1(b - 1)
                    before = {}
                    if isinstance(b, int) and b == 0 and p == 0:
                        for u in range(HT):
                            before[XT * u] = lambda u=u: dve.wait_ge(first_h[u], 16)
                    else:
                        dve.wait_ge(h_tiles_loaded[p], H_SEM * (b + p))
                    layer1(steps[p], b, p, before, behind)
                    if more_h:
                        dve.wait_ge(shift_loaded, SHIFT_SEM * (2 * b + 1 + p))
                        layer0(BLOCK[2 * p + 1], b, shift_x)

            body(0, True, True)
            body(1, True)
            with dve.Fori(2, BLOCKS - 1) as b:
                body(b, True)
            body(BLOCKS - 1, False)
            sum_cur1(BLOCKS - 1)

        @block.tensor
        def _(pe):
            def transpose(b):
                first = isinstance(b, int) and b == 0
                if not first:
                    pe.wait_ge(gathered, GATH_SEM * b)
                    if isinstance(b, int) and b == 1:
                        pe.wait_ge(first_emb_t, TCH)
                    else:
                        pe.wait_ge(emb_t_ready, b - 1)
                for c in range(TCH):
                    m = PART if c < TCH - 1 else TLAST
                    if first:
                        pe.wait_ge(first_rows[c], m)
                        if c >= 2:
                            pe.wait_ge(first_emb_t, c - 1)
                    bank, at = (c % 2, c // 2) if first else (c // 4, c % 4)
                    last = nc.tensor.transpose(ps_t[0:m, bank, at * PART:(at + 1) * PART],
                                               emb[:, c * PART:c * PART + m], ident_sb[:, :])
                    if first:
                        last.then_inc(first_transposed, 1)
                if not first:
                    last.then_inc(transposed, 1)

            def layer(phase, b, acc, whole, w_high, w_low, split, rows, behind={}):
                n, k, slot, part = begins(phase, b)
                for c in range(COUNT[phase[0]]):
                    here = prod[0:rows, (slot + c) % RING]
                    if c in SPLIT[phase[0]]:
                        i, w = SPLIT[phase[0]].index(c), split.index(c)
                        there = high[0:rows, (part + i) % HIGHS]
                        pe.wait_ge(high_made, k + i + 1)
                        passes = [(w_high[:, w, :], there), (w_low[:, w, :], there),
                                  (w_high[:, w, :], low[0:rows, (part + i) % LOWS])]
                    else:
                        pe.wait_ge(made, n + c + 1)
                        passes = [(whole(c), here)]
                    for j, (stationary, moving) in enumerate(passes):
                        if j == 2:
                            pe.wait_ge(low_made, k + i + 1)
                        for half in range(COLS // BANK):
                            cols = slice(half * BANK, (half + 1) * BANK)
                            last = nc.tensor.matmul(acc[:, cols], stationary, moving[:, cols],
                                                    start=(c == 0), stop=(c == COUNT[phase[0]] - 1))
                    last.then_inc(used, 1)
                    if c in behind:
                        behind[c]()

            def layer0(phase, b, steps_before):
                if not isinstance(steps_before, int) or steps_before:
                    pe.wait_ge(cur0_ready, steps_before)
                layer(phase, b, acc0, lambda c: w0_sb[:, c, :], w0_high, w0_low,
                      SPLIT[L0], K0)

            def layer1(phase, b, steps_before, behind):
                if not isinstance(steps_before, int) or steps_before:
                    pe.wait_ge(cur1_ready, steps_before)
                layer(phase, b, acc1, lambda c: w1_sb[:, WHOLE.index(c), :], w1_high, w1_low,
                      EITHER, PART, behind)

            def mlp1(b):
                pe.wait_ge(feat_b_ready, b + 1)
                pe.wait_ge(context_in, 16 * (b + 1))
                if not (isinstance(b, int) and b == 0):
                    pe.wait_ge(hid1_ready, b)
                for m in range(M1):
                    cols = slice(m * PART, (m + 1) * PART)
                    nc.tensor.matmul(ps_m1[:, m, :], wt1b_sb[:, cols], feat_b[:, :],
                                     start=True, stop=False)
                    if m == 0:
                        pe.wait_ge(feat_a_ready, b + 1)
                    last = nc.tensor.matmul(ps_m1[:, m, :], wt1a_sb[:, cols], feat_a[:, :],
                                            start=False, stop=True)
                last.then_inc(m1_done, 1)

            def mlp2(b):
                pe.wait_ge(hid1_ready, b + 1)
                if not (isinstance(b, int) and b == 0):
                    pe.wait_ge(y_ready, b)
                for m in range(M2):
                    for k in range(M1):
                        last = nc.tensor.matmul(ps_m2[:, m * PART:(m + 1) * PART],
                                                wt2_sb[:, k, m * PART:(m + 1) * PART],
                                                hid1[:, k, :], start=(k == 0), stop=(k == M1 - 1))
                last.then_inc(m2_done, 1)

            def mlp3(b):
                pe.wait_ge(hid2_ready, b + 1)
                for k in range(M2):
                    last = nc.tensor.matmul(ps_m2[0:1, 3 * PART:], wt3_sb[:, k:k + 1], hid2[:, k, :],
                                            start=(k == 0), stop=(k == M2 - 1))
                last.then_inc(m3_done, 1)

            pe.wait_ge(weights_in, 16 * 8)
            transpose(0)
            pe.wait_ge(weights_low, len(SPLIT[L0]) + len(EITHER))
            layer0(PROLOGUE[0], 0, 0)
            layer0(PROLOGUE[1], 0, 1)

            def body(b, more_x, more_h, mlp, first=False):
                steps = (BLOCK[0], BLOCK[2]) if more_h else LAST
                layer1(steps[0], b, 2 * b, {MLP1: lambda: mlp1(b - 1)} if mlp
                       else {NEXT_X: lambda: transpose(1)})
                if more_h:
                    layer0(BLOCK[1], b, 2 * b + 2)
                behind = {MLP2: lambda: mlp2(b - 1)} if mlp else {}
                if more_x:
                    behind[NEW_X] = lambda: transpose(b + 2)
                layer1(steps[1], b, 2 * b + 1, behind)
                if mlp:
                    mlp3(b - 1)
                if more_h:
                    layer0(BLOCK[3], b, 2 * b + 3)

            body(0, True, True, False, True)
            body(1, True, True, True)
            with pe.Fori(2, BLOCKS - 2) as b:
                body(b, True, True, True)
            body(BLOCKS - 2, False, True, True)
            body(BLOCKS - 1, False, False, True)
            mlp1(BLOCKS - 1)
            mlp2(BLOCKS - 1)
            mlp3(BLOCKS - 1)


def w0_rows():
    import numpy as np
    first = np.full((K0, N0), -1)
    second = np.full((K0, N0), -1)
    seen = set()
    for c, (t, u) in enumerate(PAIRS0):
        for q in range(3):
            for r in range(FIELDS):
                i, j = (r + SHIFTS[t][q]) % FIELDS, (r + SHIFTS[u][q]) % FIELDS
                if (min(i, j), max(i, j)) in seen:
                    continue
                seen.add((min(i, j), max(i, j)))
                first[q * FIELDS + r, c] = i * FIELDS + j
                if i != j:
                    second[q * FIELDS + r, c] = j * FIELDS + i
    assert len(seen) == FIELDS * (FIELDS + 1) // 2
    return first, second


def kernel(**inputs):
    import numpy as np
    import concourse.bacc as bacc
    from concourse.bass_utils import run_bass_kernel_spmd

    def rows_of(w, at):
        padded = np.concatenate([w, np.zeros((1, w.shape[1]), w.dtype)])
        return np.ascontiguousarray(padded[at])

    a = {k: np.asarray(v) for k, v in inputs.items()}
    ids = np.ascontiguousarray(a["ids"].reshape(BLOCKS, PART, FIELDS).transpose(1, 0, 2)).reshape(PART, -1).view(np.uint32)
    w0 = np.concatenate([a["L0_rec_W0"][:, HALF:], a["L0_rec_W0"][:, :HALF]], axis=1)
    first, second = w0_rows()
    r = np.arange(PART)
    w1_at = np.stack([np.where(8 * t + r % 8 < FIELDS, (8 * t + r % 8) * HALF + 16 * u + r // 8, -1)
                      for t, u in PAIRS1], axis=1)
    wt1 = a["W_top1"]
    arrays = {
        "ids": ids,
        "ctx_t": np.ascontiguousarray(a["dense_ctx"].T),
        "w0a": rows_of(w0, first),
        "w0b": rows_of(w0, second),
        "w1": rows_of(a["L0_rec_W1"], w1_at[:, WHOLE]),
        "w1s": rows_of(a["L0_rec_W1"], w1_at[:, EITHER]),
        "b1": np.ascontiguousarray(a["b_top1"].reshape(M1, PART).T),
        "b2": np.ascontiguousarray(a["b_top2"].reshape(M2, PART).T),
        "wt1a": np.ascontiguousarray(wt1[HALF:HALF + CH]),
        "wt1b": np.concatenate([wt1[:HALF], wt1[HALF + CH:]]),
        "wt2": np.ascontiguousarray(a["W_top2"].reshape(M1, PART, H2).transpose(1, 0, 2)),
        "wt3": np.ascontiguousarray(a["W_top3"].reshape(M2, PART).T),
        "ident": np.eye(PART, dtype=np.float32),
    }
    nc = bacc.Bacc("TRN2", target_bir_lowering=False, num_devices=1)
    fed, aps = {}, {}
    for name, x in list(arrays.items()) + [(f"tbl_{f}", a[f"tbl_{f}"]) for f in range(FIELDS)]:
        fed[f"in_{name}"] = x
        aps[name] = nc.dram_tensor(f"in_{name}", x.shape, mybir.dt.from_np(x.dtype), kind="ExternalInput").ap()
    out = nc.dram_tensor("out_y", (1, BATCH), mybir.dt.float32, kind="ExternalOutput").ap()
    tables = [aps.pop(f"tbl_{f}") for f in range(FIELDS)]
    cin_kernel(nc, tables=tables, out=out, **aps)
    got = run_bass_kernel_spmd(nc, [fed], core_ids=[0])
    return got.results[0]["out_y"].reshape(BATCH, 1)
```
